# Optimizing a Trainium2 kernel written in Bass

```python
import numpy as np
import jax
import jax.numpy as jnp

def _softmax(x, axis=-1):
    return jax.nn.softmax(x, axis=axis)

def _gelu(x):
    return jax.nn.gelu(x, approximate=True)

def _silu(x):
    return jax.nn.silu(x)

def _sigmoid(x):
    return jax.nn.sigmoid(x)

def _layernorm(x, axis=-1, eps=1e-05):
    m = jnp.mean(x, axis=axis, keepdims=True)
    v = jnp.var(x, axis=axis, keepdims=True)
    return (x - m) / jnp.sqrt(v + eps)

def _scatter_add(tgt, idx, src, axis=0):
    return tgt.at[idx].add(src)

def _segment_sum(src, seg, n):
    return jax.ops.segment_sum(src, seg, n)
kernel_name = 'mk_adj_preln_d2_adj_r2_21fa0e'

def setup_inputs(seed: int=0):
    np.random.seed(seed)
    _w = jnp.asarray

    def _rec_inputs():
        import jax
        import jax.numpy as jnp
        _gk = jax.random.key(seed)
        x = -1.394e-06 + 0.9999 * jax.random.normal(jax.random.fold_in(_gk, 1), (64, 128, 256), jnp.float32)
        _a = jax.random.bernoulli(jax.random.fold_in(_gk, 2), 0.015625, (64, 128, 128))
        adj = _a.astype(jnp.int32)
        return (x, adj)
    x, adj = _rec_inputs()

    def _L0_gnn_setup():
        import jax, jax.numpy as jnp
        import numpy as np
        NEG_INF = -1000000000.0
        NEG_SLOPE = 0.2

        def gat_layer(x, mask, W, a_src, a_dst, bias, concat):
            B, N, _ = x.shape
            H, F = a_src.shape
            xl = (x @ W).reshape(B, N, H, F)
            asrc = jnp.einsum('bnhf,hf->bnh', xl, a_src)
            adst = jnp.einsum('bnhf,hf->bnh', xl, a_dst)
            e = jax.nn.leaky_relu(asrc[:, :, None, :] + adst[:, None, :, :], NEG_SLOPE)
            e = jnp.where(mask[..., None], e, NEG_INF)
            attn = jax.nn.softmax(e, axis=1)
            out = jnp.einsum('bsdh,bshf->bdhf', attn, xl)
            if concat:
                out = out.reshape(B, N, H * F)
            else:
                out = out.mean(axis=2)
            return out + bias
        key = jax.random.key(seed)
        ks = jax.random.split(key, 10)
        B, N, Din, Fh, H, Dout = (8, 512, 256, 128, 4, 256)
        s = 0.05
        return {'adj': jax.random.randint(ks[0], (B, N, N), 0, 2, dtype=jnp.int32), 'x': jax.random.normal(ks[1], (B, N, Din), dtype=jnp.float32), 'W1': jax.random.normal(ks[2], (Din, H * Fh), dtype=jnp.float32) * s, 'att_src1': jax.random.normal(ks[3], (H, Fh), dtype=jnp.float32) * s, 'att_dst1': jax.random.normal(ks[4], (H, Fh), dtype=jnp.float32) * s, 'b1': jax.random.normal(ks[5], (H * Fh,), dtype=jnp.float32) * s, 'W2': jax.random.normal(ks[6], (H * Fh, Dout), dtype=jnp.float32) * s, 'att_src2': jax.random.normal(ks[7], (1, Dout), dtype=jnp.float32) * s, 'att_dst2': jax.random.normal(ks[8], (1, Dout), dtype=jnp.float32) * s, 'b2': jax.random.normal(ks[9], (Dout,), dtype=jnp.float32) * s}
    _L0_gnn_all = _L0_gnn_setup()
    _L0_gnn_in = {k: v for k, v in _L0_gnn_all.items() if k in ('W1', 'att_src1', 'att_dst1', 'b1', 'W2', 'att_src2', 'att_dst2', 'b2')}
    del _L0_gnn_all

    def _L1_gnn_setup():
        import jax, jax.numpy as jnp
        import numpy as np
        B, N, D = (32, 128, 256)
        DIR = 2
        NUM_LABELS = 16
        key = jax.random.key(seed)
        k1, k2, k3, k4 = jax.random.split(key, 4)
        feature = jax.random.normal(k1, (B, N, D), dtype=jnp.float32)
        graph = jax.random.randint(k2, (B, N, N), 0, NUM_LABELS, dtype=jnp.int64)
        weights = jax.random.normal(k3, (DIR, D, D), dtype=jnp.float32) * (1.0 / np.sqrt(D))
        stdv = 1.0 / np.sqrt(D)
        bias = jax.random.uniform(k4, (NUM_LABELS, D), dtype=jnp.float32, minval=-stdv, maxval=stdv)
        return {'feature': feature, 'graph': graph, 'weights': weights, 'bias': bias}
    _L1_gnn_all = _L1_gnn_setup()
    _L1_gnn_in = {k: v for k, v in _L1_gnn_all.items() if k in ('weights', 'bias')}
    del _L1_gnn_all
    return {'x': x, 'adj': adj, 'L0_gnn_W1': _L0_gnn_in['W1'], 'L0_gnn_att_src1': _L0_gnn_in['att_src1'], 'L0_gnn_att_dst1': _L0_gnn_in['att_dst1'], 'L0_gnn_b1': _L0_gnn_in['b1'], 'L0_gnn_W2': _L0_gnn_in['W2'], 'L0_gnn_att_src2': _L0_gnn_in['att_src2'], 'L0_gnn_att_dst2': _L0_gnn_in['att_dst2'], 'L0_gnn_b2': _L0_gnn_in['b2'], 'L1_gnn_weights': _L1_gnn_in['weights'], 'L1_gnn_bias': _L1_gnn_in['bias']}

def reference(x, adj, L0_gnn_W1, L0_gnn_att_src1, L0_gnn_att_dst1, L0_gnn_b1, L0_gnn_W2, L0_gnn_att_src2, L0_gnn_att_dst2, L0_gnn_b2, L1_gnn_weights, L1_gnn_bias):
    import jax
    import jax.numpy as jnp

    def _L0_gnn_ref(adj, x, W1, att_src1, att_dst1, b1, W2, att_src2, att_dst2, b2):
        import jax, jax.numpy as jnp
        import numpy as np
        NEG_INF = -1000000000.0
        NEG_SLOPE = 0.2

        def gat_layer(x, mask, W, a_src, a_dst, bias, concat):
            B, N, _ = x.shape
            H, F = a_src.shape
            xl = (x @ W).reshape(B, N, H, F)
            asrc = jnp.einsum('bnhf,hf->bnh', xl, a_src)
            adst = jnp.einsum('bnhf,hf->bnh', xl, a_dst)
            e = jax.nn.leaky_relu(asrc[:, :, None, :] + adst[:, None, :, :], NEG_SLOPE)
            e = jnp.where(mask[..., None], e, NEG_INF)
            attn = jax.nn.softmax(e, axis=1)
            out = jnp.einsum('bsdh,bshf->bdhf', attn, xl)
            if concat:
                out = out.reshape(B, N, H * F)
            else:
                out = out.mean(axis=2)
            return out + bias
        B, N, _ = adj.shape
        mask = (adj > 0) | jnp.eye(N, dtype=bool)[None]
        h = jax.nn.elu(gat_layer(x, mask, W1, att_src1, att_dst1, b1, concat=True))
        h = gat_layer(h, mask, W2, att_src2, att_dst2, b2, concat=False)
        return h

    def _L1_gnn_ref(feature, graph, weights, bias):
        import jax, jax.numpy as jnp
        import numpy as np
        B, N, D = (32, 128, 256)
        DIR = 2
        NUM_LABELS = 16
        out = feature + jnp.einsum('bni,doi->bno', feature, weights)
        out = out + jnp.take(bias, graph, axis=0).sum(axis=2)
        return out
    h = jnp.maximum(_layernorm(x, axis=-1), 0.0)
    x = x + _L0_gnn_ref(adj, h, L0_gnn_W1, L0_gnn_att_src1, L0_gnn_att_dst1, L0_gnn_b1, L0_gnn_W2, L0_gnn_att_src2, L0_gnn_att_dst2, L0_gnn_b2)
    h = jnp.maximum(_layernorm(x, axis=-1), 0.0)
    x = x + _L1_gnn_ref(h, adj, L1_gnn_weights, L1_gnn_bias)
    return x

_drawn_inputs = setup_inputs


def setup_inputs(seed=0):
    import zlib

    import numpy as np

    out = dict(_drawn_inputs(seed))
    spreads = {}
    factors = {'L0_gnn_att_src1': 7.131,
     'L0_gnn_att_dst1': 28.811,
     'L0_gnn_b1': 3.056,
     'L0_gnn_att_src2': 7.971,
     'L0_gnn_att_dst2': 36.413,
     'L0_gnn_b2': 2.821}
    for name, (base, spread) in spreads.items():
        noise = np.random.default_rng([zlib.crc32(name.encode()), seed]).standard_normal(out[name].shape)
        drawn = base * np.exp(spread * noise) if base else spread * noise
        out[name] = jnp.asarray(drawn.astype(out[name].dtype))
    for name, factor in factors.items():
        out[name] = (out[name] * factor).astype(out[name].dtype)
    return out
```

```python
import concourse.bass as bass
from concourse import mybir
from contextlib import ExitStack


def gat_graphconv_block(
    nc: bass.Bass,
    x: bass.AP,
    adj: bass.AP,
    W1: bass.AP,
    att_src1: bass.AP,
    att_dst1: bass.AP,
    b1: bass.AP,
    W2: bass.AP,
    att_src2: bass.AP,
    att_dst2: bass.AP,
    b2: bass.AP,
    W3: bass.AP,
    label_bias: bass.AP,
    out: bass.AP,
):
    F32 = mybir.dt.float32
    F32R = mybir.dt.float32r
    BF16 = mybir.dt.bfloat16
    I32 = mybir.dt.int32
    ALU = mybir.AluOpType
    ACT = mybir.ActivationFunctionType
    AX = mybir.AxisListType

    G, N, D = x.shape
    H, FH = att_src1.shape
    HF = H * FH
    KD = D // 128
    KH = HF // 128
    HALF = HF // 2
    C1 = HALF + 4
    C2 = D + 2
    SLOPE = 0.2
    EPS = 1e-5
    NEG = -float(2 ** 32)
    LO = 32
    RW = LO + 8
    CW = 72
    AHEAD = 8

    x_v = x.rearrange("g n c -> n g c")
    out_v = out.rearrange("g n c -> n g c")
    adj_v = adj.rearrange("g s d -> s g d")

    def row_of(h):
        return 4 * (h // 2) + h % 2

    def pipeline(eng, steps):
        lags = [lag for _, lag in steps]
        lo = max(lags) + 2 + max(lags) % 2
        hi = G + min(lags)
        hi -= (hi - lo) % 2

        def slot(t, parity):
            for stage, lag in steps:
                g = t - lag
                if not isinstance(g, int) or 0 <= g < G:
                    stage(g, (parity + lag) % 2)

        for t in range(min(lags), lo):
            slot(t, t % 2)
        with eng.Fori(lo // 2, hi // 2) as turn:
            slot(2 * turn, 0)
            slot(2 * turn + 1, 1)
        for t in range(hi, G + max(lags)):
            slot(t, t % 2)

    with ExitStack() as ctx:
        def sb(name, shape, dt=F32):
            return ctx.enter_context(nc.sbuf_tensor(name, shape, dt))

        def pb(name, shape):
            return ctx.enter_context(nc.psum_tensor(name, shape, F32))

        def sem(name):
            return ctx.enter_context(nc.semaphore(name))

        def two(name, shape, dt=F32):
            return [sb(f"{name}{p}", shape, dt) for p in range(2)]

        x_all = sb("x_all", [128, G * D])
        adj_all = sb("adj_all", [128, G * N], I32)
        mask_all = sb("mask_all", [128, G * N], BF16)
        n0_all = sb("n0_all", [128, G])
        w1_hi = sb("w1_hi", [128, KD, 2, C1], F32R)
        w1_lo = sb("w1_lo", [128, KD, 2, C1], F32R)
        w2_hi = sb("w2_hi", [128, KH, C2], F32R)
        w2_lo = sb("w2_lo", [128, KH, C2], F32R)
        w3_hi = sb("w3_hi", [128, KD, D], F32R)
        w3_lo = sb("w3_lo", [128, KD, D], F32R)
        b1_bc = sb("b1_bc", [128, HF])
        b2_bc = sb("b2_bc", [128, D])
        ident = sb("ident", [128, 128])
        ident_bf = sb("ident_bf", [128, 128], BF16)
        off_diag = sb("off_diag", [128, 128], BF16)
        sel_src1 = sb("sel_src1", [RW, H, 128], F32R)
        sel_dst1 = sb("sel_dst1", [RW, H, 128], F32R)
        sel_src2 = sb("sel_src2", [RW, 128], F32R)
        sel_dst2 = sb("sel_dst2", [RW, 128], F32R)
        label_rows = sb("label_rows", [RW, D], F32R)
        minus_half = sb("minus_half", [128, 2])
        eps_col = sb("eps_col", [128, 2])

        staged = [G * D]

        def stage(*shape):
            size = 1
            for n in shape:
                size *= n
            staged[0] -= size
            names = "abc"[:len(shape)]
            return x_all[:, staged[0]:staged[0] + size].rearrange(
                f"p ({' '.join(names)}) -> p {' '.join(names)}", **dict(zip(names, shape)))

        w1_f = stage(KD, HF)
        w2_f = stage(KH, D)
        w3_f = stage(2, KD * D).rearrange("p j (k i) -> p j k i", k=KD)
        w1_cat = stage(KD, 2 * C1).rearrange("p k (a n) -> p k a n", a=2)
        w2_cat = stage(KH, C2)
        att1_bc = stage(2, HF)
        att2_bc = stage(2, D)
        w_att = stage(1, HF)[:, 0, :]
        lab = stage(2, D)[0:1]
        lab_f = stage(2, D)[0:1]
        assert staged[0] >= (AHEAD + 2) * 2 * D
        fold = sb("fold", [RW, 8])
        lab_parts = sb("lab_parts", [1, 4, D], F32R)

        hn = two("hn", [128, D])
        hT_hi = two("hT_hi", [128, KD, 128], F32R)
        hT_lo = two("hT_lo", [128, KD, 128], F32R)
        xl = two("xl", [128, HF])
        ab1 = two("ab1", [128, CW], F32R)
        rows1 = two("rows1", [RW, 128], F32R)
        L1 = two("L1", [128, H, 128])
        nmax1 = two("nmax1", [128, H])
        sum1 = two("sum1", [128, H])
        rsum1 = two("rsum1", [128, H])
        P1 = two("P1", [128, H, 128])
        PT1 = two("PT1", [128, H, 128])
        elu_e = two("elu_e", [128, HF])
        h1 = two("h1", [128, HF])
        h1_hi = two("h1_hi", [128, KH, 128], F32R)
        h1_lo = two("h1_lo", [128, KH, 128], F32R)
        ab2 = two("ab2", [128, CW], F32R)
        xl2 = two("xl2", [128, D])
        rows2 = two("rows2", [RW, 128], F32R)
        L2 = two("L2", [128, 128])
        nmax2 = two("nmax2", [128, 1])
        sum2 = two("sum2", [128, 1])
        rsum2 = two("rsum2", [128, 1])
        P2 = two("P2", [128, 128])
        PT2 = two("PT2", [128, 128])
        h2n = two("h2n", [128, D])
        h2T_hi = two("h2T_hi", [128, KD, 128], F32R)
        h2T_lo = two("h2T_lo", [128, KD, 128], F32R)
        bn1 = sb("bn1", [128, 2, 6])
        mv1 = sb("mv1", [128, 2, 2])
        ve1 = sb("ve1", [128, 2])
        rstd1 = sb("rstd1", [128, 2])
        bn2 = sb("bn2", [128, 6])
        mv2 = two("mv2", [128, 2])
        ve2 = sb("ve2", [128, 1])
        rstd2 = sb("rstd2", [128, 1])

        pX = pb("pX", [128, 2, 512])
        pZ = pb("pZ", [128, 512])
        pP = pb("pP", [128, H, 128])
        pA = pb("pA", [128, 512])
        pY = pb("pY", [128, 512])
        pS = pb("pS", [128, 512])
        pT = pb("pT", [128, 512])
        s_L1, s_L2 = sem("leaky1"), sem("leaky2")
        loads = {k: [sem(f"{k}_dma{q}") for q in range(2)] for k in ("x", "adj")}
        s_loaded = sem("loaded")
        s_w1dma, s_w2dma, s_w3dma, s_labdma, s_labrow = (sem(n) for n in ("w1dma", "w2dma", "w3dma", "labdma", "labrow"))
        s_ident, s_consts, s_prep, s_w3T, s_w3ready = (sem(n) for n in ("ident", "consts", "prep", "w3T", "w3ready"))
        s_bn1, s_mv1, s_rs1a, s_rs1, s_hn = (sem(n) for n in ("bn1_done", "mv1_done", "rs1a", "rs1", "hn_done"))
        s_m0, s_n0, s_mask = sem("mask_raw"), sem("n0_done"), sem("mask_done")
        s_T0, s_hThi, s_hTlo = sem("T0"), sem("hThi"), sem("hTlo")
        s_xl1, s_ab1hi, s_ab1, s_xlsb = sem("xl1"), sem("ab1hi"), sem("ab1_done"), sem("xl_sb")
        s_R1, s_rows1, s_z1, s_sc1, s_max1, s_exp1, s_rsum1, s_P1 = (
            sem(n) for n in ("R1", "rows1_sb", "z1", "scaled1", "max1", "exp1", "rsum1_done", "P1_done"))
        s_PT, s_PT1, s_attn1, s_E, s_elu_a, s_h1, s_h1hi, s_h1lo = (
            sem(n) for n in ("PT", "PT1_sb", "attn1", "elu_exp", "elu_a", "h1_done", "h1hi", "h1lo"))
        s_xl2, s_ab2hi, s_n0col, s_ab2, s_xl2sb = sem("xl2"), sem("ab2hi"), sem("n0col"), sem("ab2_done"), sem("xl2_sb")
        s_R2, s_rows2, s_z2, s_sc2, s_max2, s_exp2, s_rsum2, s_P2 = (
            sem(n) for n in ("R2", "rows2_sb", "z2", "scaled2", "max2", "exp2", "rsum2_done", "P2_done"))
        s_P2T, s_PT2, s_attn2, s_x2, s_bn2, s_mv2, s_rs2a, s_rs2, s_h2n = (
            sem(n) for n in ("P2T", "PT2_sb", "attn2", "x2", "bn2_done", "mv2_done", "rs2a", "rs2", "h2n_done"))
        s_T2, s_h2hi, s_h2lo, s_fin, s_out, s_stored = (
            sem(n) for n in ("T2", "h2hi", "h2lo", "final", "out_done", "stored"))

        block = ctx.enter_context(nc.Block())

        def of_graph(tile, g, width, graphs=1):
            return tile[:, bass.ds(g * width, graphs * width)]

        @block.sync
        def _(sp):
            def load(g, p):
                if p:
                    return
                q = q_of[0] % 2
                q_of[0] += 1
                sp.dma_start(of_graph(x_all, g, D, 2).rearrange("n (g c) -> n g c", g=2),
                             x_v[:, bass.ds(g, 2), :]).then_inc(loads["x"][0], 16)
                sp.dma_start(of_graph(adj_all, g, N, 2).rearrange("n (g c) -> n g c", g=2),
                             adj_v[:, bass.ds(g, 2), :]).then_inc(loads["adj"][0], 16)
                sp.wait_ge(loads["x"][0], 8 * g + 16)
                sp.wait_ge(loads["adj"][0], 8 * g + 16)
                sp.sem_inc(s_loaded, 2)

            q_of = [0]

            def store(g, p):
                if not p:
                    return
                sp.wait_ge(s_out, g + 1)
                sp.dma_start(out_v[:, bass.ds(g - 1, 2), :],
                             of_graph(x_all, g - 1, D, 2).rearrange("n (g c) -> n g c", g=2)).then_inc(s_stored, 16)

            pipeline(sp, [(load, -AHEAD), (store, 6)])
            sp.wait_ge(s_stored, 16 * (G // 2))

        @block.gpsimd
        def _(pool):
            pool.memset(ident[:, :], 0.0).then_inc(s_ident, 1)
            pool.memset(off_diag[:, :], 1.0).then_inc(s_ident, 1)
            pool.memset(minus_half[:, :], -0.5).then_inc(s_ident, 1)
            pool.memset(eps_col[:, :], EPS).then_inc(s_ident, 1)
            pool.wait_ge(s_ident, 4)
            pool.affine_select(out=ident[:, :], in_=ident[:, :], compare_op=ALU.not_equal, fill=1.0,
                               base=0, pattern=[[-1, 128]], channel_multiplier=1).then_inc(s_ident, 1)
            pool.affine_select(out=off_diag[:, :], in_=off_diag[:, :], compare_op=ALU.not_equal, fill=0.0,
                               base=0, pattern=[[-1, 128]], channel_multiplier=1).then_inc(s_ident, 1)

            def inverse_std1(g, p):
                if p:
                    return
                pool.wait_ge(s_mv1, g + 2)
                pool.tensor_tensor(ve1[:, :], mv1[:, :, 1], eps_col[:, :], ALU.add).then_inc(s_rs1a, 2)
                pool.wait_ge(s_rs1a, g + 2)
                pool.tensor_tensor(rstd1[:, :], ve1[:, :], minus_half[:, :], ALU.pow).then_inc(s_rs1, 2)

            def split_h1(g, p):
                pool.wait_ge(s_h1hi, g + 1)
                pool.tensor_tensor(h1_lo[p][:, :, :].rearrange("p a b -> p (a b)"), h1[p][:, :],
                                   h1_hi[p][:, :, :].rearrange("p a b -> p (a b)").bitcast(F32),
                                   ALU.subtract).then_inc(s_h1lo, 1)

            def inverse_std2(g, p):
                pool.wait_ge(s_mv2, g + 1)
                if not isinstance(g, int) or g >= 1:
                    pool.wait_ge(s_h2n, g)
                pool.tensor_tensor(ve2[:, :], mv2[p][:, 1:2], eps_col[:, 0:1], ALU.add).then_inc(s_rs2a, 1)
                pool.wait_ge(s_rs2a, g + 1)
                pool.tensor_tensor(rstd2[:, :], ve2[:, :], minus_half[:, 0:1], ALU.pow).then_inc(s_rs2, 1)

            def normalise1(g, p):
                pool.wait_ge(s_rsum1, g + 1)
                if not isinstance(g, int) or g >= 2:
                    pool.wait_ge(s_PT, g - 1)
                pool.tensor_tensor(P1[p][:, :, :], L1[p][:, :, :],
                                   rsum1[p][:, :].unsqueeze(2).broadcast_to([128, H, 128]), ALU.mult).then_inc(s_P1, 1)

            pipeline(pool, [(split_h1, 2), (inverse_std2, 4), (inverse_std1, -2), (normalise1, 0)])

        @block.scalar
        def _(act):
            act.dma_start(w1_f[:, :, :], W1.rearrange("(k p) n -> p k n", p=128)).then_inc(s_w1dma, 16)
            for j, a in enumerate((att_src1, att_dst1)):
                act.dma_start(att1_bc[:, j, :], a.rearrange("h f -> (h f)").unsqueeze(0).broadcast_to([128, HF])).then_inc(s_w1dma, 16)
            act.dma_start(b1_bc[:, :], b1.unsqueeze(0).broadcast_to([128, HF])).then_inc(s_w1dma, 16)
            act.dma_start(w2_f[:, :, :], W2.rearrange("(k p) n -> p k n", p=128)).then_inc(s_w2dma, 16)
            for j, a in enumerate((att_src2, att_dst2)):
                act.dma_start(att2_bc[:, j, :], a.broadcast_to([128, D])).then_inc(s_w2dma, 16)
            act.dma_start(b2_bc[:, :], b2.unsqueeze(0).broadcast_to([128, D])).then_inc(s_w2dma, 16)
            for j in range(2):
                act.dma_start(w3_f[:, j, :, :], W3[j].rearrange("(k o) i -> o k i", o=128)).then_inc(s_w3dma, 16)
            act.dma_start(lab[:, :, :], label_bias[0:2, :].unsqueeze(0)).then_inc(s_labdma, 16)

            act.wait_ge(s_consts, 1)
            act.wait_ge(s_w3ready, 2)
            for j in range(2):
                act.dma_start(label_rows[LO * j + 2:LO * j + 4, :].bitcast(F32),
                              lab_parts[:, 2 * j:2 * j + 2, :].bitcast(F32)).then_inc(s_labrow, 16)

            def relu_h(g, p):
                act.wait_ge(s_T0, g + 1)
                if not isinstance(g, int) or g >= 2:
                    act.wait_ge(s_xl1, g - 1)
                act.activation(hT_hi[p][:, :, :], pS[:, 0:D].rearrange("p (k n) -> p k n", k=KD), ACT.Relu).then_inc(s_hThi, 1)

            def score_rows1(g, p):
                act.wait_ge(s_R1, g + 1)
                act.activation(rows1[p][:, :], pT[0:RW, 128:256], ACT.Copy).then_inc(s_rows1, 1)

            def scaled1(g, p):
                act.wait_ge(s_z1, g + 1)
                if not isinstance(g, int) or g >= 2:
                    act.wait_ge(s_P1, g - 1)
                act.activation(L1[p][:, :, :].rearrange("p h s -> p (h s)"), pZ[:, :], ACT.Copy, scale=SLOPE).then_inc(s_sc1, 1)

            def exp1(g, p):
                act.wait_ge(s_max1, g + 1)
                for h in range(H):
                    last = act.activation(L1[p][:, h, :], L1[p][:, h, :], ACT.Exp, bias=nmax1[p][:, h:h + 1],
                                          accum_out=sum1[p][:, h:h + 1])
                last.then_inc(s_exp1, 1)

            def copy_PT1(g, p):
                act.wait_ge(s_PT, g + 1)
                if not isinstance(g, int) or g >= 2:
                    act.wait_ge(s_attn1, g - 1)
                act.activation(PT1[p][:, :, :], pP[:, :, :], ACT.Copy).then_inc(s_PT1, 1)

            def elu_exp(g, p):
                act.wait_ge(s_attn1, g + 1)
                if not isinstance(g, int) or g >= 2:
                    act.wait_ge(s_h1, g - 1)
                act.activation(elu_e[p][:, :], pA[:, :], ACT.Exp).then_inc(s_E, 1)

            def score_rows2(g, p):
                act.wait_ge(s_R2, g + 1)
                if not isinstance(g, int) or g >= 2:
                    act.wait_ge(s_fin, g - 1)
                act.activation(rows2[p][:, :], pS[0:RW, 256:384], ACT.Copy).then_inc(s_rows2, 1)

            def scaled2(g, p):
                act.wait_ge(s_z2, g + 1)
                if not isinstance(g, int) or g >= 2:
                    act.wait_ge(s_P2, g - 1)
                act.activation(L2[p][:, :], pT[:, 256:384], ACT.Copy, scale=SLOPE).then_inc(s_sc2, 1)

            def exp2(g, p):
                act.wait_ge(s_max2, g + 1)
                act.activation(L2[p][:, :], L2[p][:, :], ACT.Exp, bias=nmax2[p][:, :],
                               accum_out=sum2[p][:, :]).then_inc(s_exp2, 1)

            def copy_PT2(g, p):
                act.wait_ge(s_P2T, g + 1)
                if not isinstance(g, int) or g >= 2:
                    act.wait_ge(s_attn2, g - 1)
                act.activation(PT2[p][:, :], pT[:, 0:128], ACT.Copy).then_inc(s_PT2, 1)

            def relu_h2(g, p):
                act.wait_ge(s_T2, g + 1)
                if not isinstance(g, int) or g >= 2:
                    act.wait_ge(s_fin, g - 1)
                act.activation(h2T_hi[p][:, :, :], pS[:, 0:D].rearrange("p (k n) -> p k n", k=KD), ACT.Relu).then_inc(s_h2hi, 1)

            pipeline(act, [(relu_h2, 5), (copy_PT2, 4), (score_rows1, 0), (copy_PT1, 1), (score_rows2, 3),
                           (scaled1, 0), (relu_h, -1), (scaled2, 3), (exp1, 0), (exp2, 3), (elu_exp, 1)])

        @block.vector
        def _(dve):
            prep = [0]

            def link(ins):
                prep[0] += 1
                ins.then_inc(s_prep, 1)
                dve.wait_ge(s_prep, prep[0])

            for p in range(2):
                dve.memset(ab1[p][:, :].bitcast(F32), 0.0)
                dve.memset(ab2[p][:, :].bitcast(F32), 0.0)
            dve.memset(label_rows[:, :].bitcast(F32), 0.0).then_inc(s_consts, 1)
            dve.wait_ge(s_w1dma, 64)
            for k in range(KD):
                for j in range(2):
                    link(dve.tensor_tensor(w_att[:, :], w1_f[:, k, :], att1_bc[:, j, :], ALU.mult))
                    link(dve.tensor_reduce(w1_cat[:, k, :, HALF + 2 * j:HALF + 2 * j + 2],
                                           w_att[:, :].rearrange("p (a h f) -> p a h f", a=2, h=2), AX.X, ALU.add))
            for k in range(KD):
                link(dve.tensor_copy(w1_cat[:, k, :, 0:HALF], w1_f[:, k, :].rearrange("p (a n) -> p a n", a=2)))
                link(dve.tensor_copy(w1_hi[:, k, :, :], w1_cat[:, k, :, :]))
                link(dve.tensor_tensor(w1_lo[:, k, :, :], w1_cat[:, k, :, :], w1_hi[:, k, :, :].bitcast(F32), ALU.subtract))
            dve.wait_ge(s_ident, 6)
            link(dve.tensor_copy(ident_bf[:, :], ident[:, :]))
            link(dve.tensor_tensor(fold[:, :], ident[0:RW, 0:8], ident[0:RW, LO:LO + 8], ALU.add))
            for h in range(H):
                r = row_of(h)
                dve.tensor_copy(sel_src1[:, h, :], fold[:, r:r + 1].broadcast_to([RW, 128]))
                link(dve.tensor_copy(sel_dst1[:, h, :], fold[:, r + 2:r + 3].broadcast_to([RW, 128])))
            dve.tensor_copy(sel_src2[:, :], fold[:, 0:1].broadcast_to([RW, 128]))
            link(dve.tensor_copy(sel_dst2[:, :], fold[:, 1:2].broadcast_to([RW, 128])))
            for p in range(2):
                link(dve.memset(ab2[p][:, 3:RW:LO].bitcast(F32), 1.0))
            dve.tensor_copy(ident_bf[:, 0:1], ident[:, 0:1]).then_inc(s_consts, 1)

            def late_weights():
                dve.wait_ge(s_w2dma, 64)
                for k in range(KH):
                    for j in range(2):
                        link(dve.tensor_tensor(w_att[:, 0:D], w2_f[:, k, :], att2_bc[:, j, :], ALU.mult))
                        link(dve.tensor_reduce(w2_cat[:, k, D + j:D + j + 1], w_att[:, 0:D], AX.X, ALU.add))
                link(dve.tensor_copy(w2_cat[:, :, 0:D], w2_f[:, :, :]))
                link(dve.tensor_copy(w2_hi[:, :, :], w2_cat[:, :, :]))
                link(dve.tensor_tensor(w2_lo[:, :, :], w2_cat[:, :, :], w2_hi[:, :, :].bitcast(F32), ALU.subtract))
                dve.wait_ge(s_w3dma, 32)
                link(dve.tensor_tensor(w3_f[:, 0, :, :], w3_f[:, 0, :, :], w3_f[:, 1, :, :], ALU.add))
                for k in range(KD):
                    link(dve.tensor_tensor(w3_f[:, 0, k, k * 128:(k + 1) * 128], w3_f[:, 0, k, k * 128:(k + 1) * 128],
                                           ident[:, :], ALU.add))
                dve.tensor_copy(ident_bf[:, 0:1], ident[:, 0:1]).then_inc(s_w3ready, 1)
                dve.wait_ge(s_labdma, 16)
                link(dve.tensor_tensor(lab_f[:, 0, :], lab[:, 0, :], lab[:, 1, :], ALU.subtract))
                link(dve.tensor_scalar(lab_f[:, 0, :], lab_f[:, 0, :], 1.0 / NEG, None, ALU.mult))
                link(dve.tensor_scalar(lab_f[:, 1, :], lab[:, 1, :], float(N), None, ALU.mult))
                link(dve.tensor_copy(lab_parts[:, 0:2, :], lab_f[:, :, :]))
                dve.tensor_tensor(lab_parts[:, 2:4, :], lab_f[:, :, :], lab_parts[:, 0:2, :].bitcast(F32),
                                  ALU.subtract).then_inc(s_w3ready, 1)
                dve.wait_ge(s_w3T, 1)
                w3T = pZ[:, :].rearrange("p (k o) -> p k o", k=KD)
                link(dve.tensor_copy(w3_hi[:, :, :], w3T))
                dve.tensor_tensor(w3_lo[:, :, :], w3T, w3_hi[:, :, :].bitcast(F32), ALU.subtract).then_inc(s_w3ready, 1)

            def stats1(g, p):
                if p:
                    return
                dve.wait_ge(s_ident, 6)
                dve.wait_ge(s_loaded, g + 2)
                for j in range(2):
                    dve.bn_stats(bn1[:, j, :], of_graph(x_all, g + j, D)).then_inc(s_bn1, 1)
                pair = of_graph(mask_all, g, N, 2)
                dve.tensor_scalar(pair, of_graph(adj_all, g, N, 2), 0.0, NEG, ALU.is_le, ALU.mult).then_inc(s_m0, 2)
                dve.wait_ge(s_ident, 6)
                dve.wait_ge(s_bn1, g + 2)
                if not isinstance(g, int) or g >= 2:
                    dve.wait_ge(s_hn, g)
                dve.bn_aggr(mv1[:, 0, :], bn1[:, 0, :])
                dve.bn_aggr(mv1[:, 1, :], bn1[:, 1, :]).then_inc(s_mv1, 2)
                dve.wait_ge(s_m0, g + 2)
                dve.tensor_reduce(n0_all[:, bass.ds(g, 2)], pair.rearrange("p (g d) -> p g d", g=2), AX.X, ALU.add).then_inc(s_n0, 2)
                dve.wait_ge(s_n0, g + 2)
                dve.tensor_tensor(pair.rearrange("p (g d) -> p g d", g=2), pair.rearrange("p (g d) -> p g d", g=2),
                                  off_diag[:, :].unsqueeze(1).broadcast_to([128, 2, 128]), ALU.mult).then_inc(s_mask, 2)

            def layer_norm1(g, p):
                dve.wait_ge(s_rs1, g + 1)
                if not isinstance(g, int) or g >= 2:
                    dve.wait_ge(s_T0, g - 1)
                dve.tensor_scalar(hn[p][:, :], of_graph(x_all, g, D), mv1[:, p, 0:1], rstd1[:, p:p + 1],
                                  ALU.subtract, ALU.mult).then_inc(s_hn, 1)

            def layer_norm2(g, p):
                dve.wait_ge(s_rs2, g + 1)
                if not isinstance(g, int) or g >= 2:
                    dve.wait_ge(s_T2, g - 1)
                dve.tensor_scalar(h2n[p][:, :], of_graph(x_all, g, D), mv2[p][:, 0:1], rstd2[:, :],
                                  ALU.subtract, ALU.mult).then_inc(s_h2n, 1)

            def low_h(g, p):
                dve.wait_ge(s_hThi, g + 1)
                dve.scalar_tensor_tensor(hT_lo[p][:, :, :], pS[:, 0:D].rearrange("p (k n) -> p k n", k=KD), 0.0,
                                         hT_hi[p][:, :, :].bitcast(F32), ALU.max, ALU.subtract).then_inc(s_hTlo, 1)

            def scores1(g, p):
                dve.wait_ge(s_xl1, g + 1)
                cols = pX[:, :, HALF:C1]
                hi = ab1[p][:, 0:8].rearrange("p (a c) -> p a c", a=2)
                dve.tensor_copy(hi, cols).then_inc(s_ab1hi, 1)
                dve.wait_ge(s_ab1hi, g + 1)
                dve.tensor_tensor(ab1[p][:, LO:LO + 8].rearrange("p (a c) -> p a c", a=2), cols, hi.bitcast(F32),
                                  ALU.subtract).then_inc(s_ab1, 1)

            def features1(g, p):
                if not isinstance(g, int) or g >= 2:
                    dve.wait_ge(s_attn1, g - 1)
                dve.tensor_tensor(xl[p][:, :].rearrange("p (a n) -> p a n", a=2), pX[:, :, 0:HALF],
                                  b1_bc[:, :].rearrange("p (a n) -> p a n", a=2), ALU.add).then_inc(s_xlsb, 1)

            def max1(g, p):
                dve.wait_ge(s_sc1, g + 1)
                dve.tensor_tensor(L1[p][:, :, :].rearrange("p h s -> p (h s)"), pZ[:, :],
                                  L1[p][:, :, :].rearrange("p h s -> p (h s)"), ALU.max).then_inc(s_L1, 1)
                dve.wait_ge(s_L1, g + 1)
                dve.tensor_reduce(nmax1[p][:, :], L1[p][:, :, :], AX.X, ALU.max, negate=True).then_inc(s_max1, 1)

            def recip1(g, p):
                dve.wait_ge(s_exp1, g + 1)
                dve.reciprocal(rsum1[p][:, :], sum1[p][:, :]).then_inc(s_rsum1, 1)

            def elu(g, p):
                dve.wait_ge(s_E, g + 1)
                dve.tensor_scalar(elu_e[p][:, :], elu_e[p][:, :], 1.0, -1.0, ALU.min, ALU.add).then_inc(s_elu_a, 1)
                dve.wait_ge(s_elu_a, g + 1)
                if not isinstance(g, int) or g >= 2:
                    dve.wait_ge(s_h1lo, g - 1)
                dve.tensor_tensor(h1[p][:, :], pA[:, :], elu_e[p][:, :], ALU.max).then_inc(s_h1, 1)
                dve.wait_ge(s_h1, g + 1)
                if not isinstance(g, int) or g >= 2:
                    dve.wait_ge(s_xl2, g - 1)
                dve.tensor_copy(h1_hi[p][:, :, :].rearrange("p a b -> p (a b)"), h1[p][:, :]).then_inc(s_h1hi, 1)

            def scores2(g, p):
                dve.wait_ge(s_xl2, g + 1)
                dve.tensor_copy(ab2[p][:, 0:2], pY[:, D:C2]).then_inc(s_ab2hi, 1)
                dve.tensor_copy(ab2[p][:, 2:RW:LO], of_graph(n0_all, g, 1).broadcast_to([128, 2])).then_inc(s_n0col, 1)
                dve.wait_ge(s_ab2hi, g + 1)
                dve.tensor_tensor(ab2[p][:, LO:LO + 2], pY[:, D:C2], ab2[p][:, 0:2].bitcast(F32),
                                  ALU.subtract).then_inc(s_ab2, 1)
                if not isinstance(g, int) or g >= 2:
                    dve.wait_ge(s_attn2, g - 1)
                dve.tensor_tensor(xl2[p][:, :], pY[:, 0:D], b2_bc[:, :], ALU.add).then_inc(s_xl2sb, 1)

            def max2(g, p):
                dve.wait_ge(s_sc2, g + 1)
                dve.tensor_tensor(L2[p][:, :], pT[:, 256:384], L2[p][:, :], ALU.max).then_inc(s_L2, 1)
                dve.wait_ge(s_L2, g + 1)
                dve.tensor_reduce(nmax2[p][:, :], L2[p][:, :], AX.X, ALU.max, negate=True).then_inc(s_max2, 1)

            def normalise2(g, p):
                dve.wait_ge(s_exp2, g + 1)
                dve.reciprocal(rsum2[p][:, :], sum2[p][:, :]).then_inc(s_rsum2, 1)
                dve.wait_ge(s_rsum2, g + 1)
                if not isinstance(g, int) or g >= 2:
                    dve.wait_ge(s_P2T, g - 1)
                dve.tensor_scalar(P2[p][:, :], L2[p][:, :], rsum2[p][:, :], None, ALU.mult).then_inc(s_P2, 1)

            def residual1(g, p):
                dve.wait_ge(s_attn2, g + 1)
                dve.tensor_tensor(of_graph(x_all, g, D), pY[:, 0:D], of_graph(x_all, g, D), ALU.add).then_inc(s_x2, 1)
                dve.wait_ge(s_ident, 6)
                dve.wait_ge(s_x2, g + 1)
                dve.bn_stats(bn2[:, :], of_graph(x_all, g, D)).then_inc(s_bn2, 1)
                dve.wait_ge(s_ident, 6)
                dve.wait_ge(s_bn2, g + 1)
                if not isinstance(g, int) or g >= 2:
                    dve.wait_ge(s_h2n, g - 1)
                dve.bn_aggr(mv2[p][:, :], bn2[:, :]).then_inc(s_mv2, 1)

            def low_h2(g, p):
                dve.wait_ge(s_h2hi, g + 1)
                dve.scalar_tensor_tensor(h2T_lo[p][:, :, :], pS[:, 0:D].rearrange("p (k n) -> p k n", k=KD), 0.0,
                                         h2T_hi[p][:, :, :].bitcast(F32), ALU.max, ALU.subtract).then_inc(s_h2lo, 1)

            def residual2(g, p):
                dve.wait_ge(s_fin, g + 1)
                dve.wait_ge(s_h2n, g + 1)
                dve.tensor_tensor(of_graph(x_all, g, D), pZ[:, 0:D], of_graph(x_all, g, D), ALU.add).then_inc(s_out, 1)

            late_weights()
            pipeline(dve, [(low_h2, 5), (scores1, 0), (features1, 0), (elu, 2), (residual2, 5), (residual1, 4),
                           (max1, 0), (layer_norm2, 4), (low_h, -1), (max2, 3), (layer_norm1, -2), (stats1, -3), (recip1, 0),
                           (normalise2, 3), (scores2, 2)])

        @block.tensor
        def _(pe):
            pe.wait_ge(s_w3ready, 1)
            for ki in range(KD):
                for ko in range(KD):
                    mm = pe.transpose(pZ[:, ki * D + ko * 128:ki * D + (ko + 1) * 128],
                                      w3_f[:, 0, ko, ki * 128:(ki + 1) * 128], ident[:, :])
            mm.then_inc(s_w3T, 1)
            pe.wait_ge(s_consts, 2)
            pe.wait_ge(s_w3ready, 3)
            pe.wait_ge(s_labrow, 32)

            def transpose_h(g, p):
                pe.wait_ge(s_hn, g + 1)
                if not isinstance(g, int) or g >= 4:
                    pe.wait_ge(s_rows2, g - 3)
                if not isinstance(g, int) or g >= 1:
                    pe.wait_ge(s_hTlo, g)
                for k in range(KD):
                    mm = pe.transpose(pS[:, k * 128:(k + 1) * 128], hn[p][:, k * 128:(k + 1) * 128], ident[:, :])
                mm.then_inc(s_T0, 1)

            def project1(g, p):
                pe.wait_ge(s_hTlo, g + 1)
                if not isinstance(g, int) or g >= 1:
                    pe.wait_ge(s_xlsb, g)
                for a in range(2):
                    for k in range(KD):
                        pe.matmul(pX[:, a, 0:C1], hT_hi[p][:, k, :], w1_hi[:, k, a, :], start=(k == 0), stop=False)
                        pe.matmul(pX[:, a, 0:C1], hT_hi[p][:, k, :], w1_lo[:, k, a, :], start=False, stop=False)
                        mm = pe.matmul(pX[:, a, 0:C1], hT_lo[p][:, k, :], w1_hi[:, k, a, :], start=False, stop=(k == KD - 1))
                mm.then_inc(s_xl1, 1)

            def transpose_scores1(g, p):
                pe.wait_ge(s_ab1, g + 1)
                if not isinstance(g, int) or g >= 4:
                    pe.wait_ge(s_PT2, g - 3)
                pe.transpose(pT[0:CW, 128:256], ab1[p][:, :].bitcast(F32), ident[:, :]).then_inc(s_R1, 1)

            def scores1(g, p):
                pe.wait_ge(s_mask, g + 1)
                pe.wait_ge(s_rows1, g + 1)
                if not isinstance(g, int) or g >= 5:
                    pe.wait_ge(s_out, g - 4)
                if not isinstance(g, int) or g >= 1:
                    pe.wait_ge(s_L1, g)
                pe.matmul(pZ[:, :].rearrange("p (h s) -> p h s", h=H), of_graph(mask_all, g, N),
                          ident_bf[:, :].unsqueeze(1).broadcast_to([128, H, 128]), start=True, stop=False)
                pe.matmul(pZ[:, :], rows1[p][:, :], sel_dst1[:, :, :].rearrange("p h s -> p (h s)"), start=False, stop=False)
                for h in range(H):
                    mm = pe.matmul(pZ[:, h * 128:(h + 1) * 128], sel_src1[:, h, :], rows1[p][:, :], start=False, stop=(h == H - 1))
                mm.then_inc(s_z1, 1)

            def transpose_P1(g, p):
                pe.wait_ge(s_P1, g + 1)
                if not isinstance(g, int) or g >= 1:
                    pe.wait_ge(s_PT1, g)
                for h in range(H):
                    mm = pe.transpose(pP[:, h, :], P1[p][:, h, :], ident[:, :])
                mm.then_inc(s_PT, 1)

            def attend1(g, p):
                pe.wait_ge(s_PT1, g + 1)
                pe.wait_ge(s_xlsb, g + 1)
                if not isinstance(g, int) or g >= 1:
                    pe.wait_ge(s_h1, g)
                for h in range(H):
                    mm = pe.matmul(pA[:, h * 128:(h + 1) * 128], xl[p][:, h * FH:(h + 1) * FH], PT1[p][:, h, :],
                                   start=True, stop=True)
                mm.then_inc(s_attn1, 1)

            def project2(g, p):
                pe.wait_ge(s_h1lo, g + 1)
                if not isinstance(g, int) or g >= 1:
                    pe.wait_ge(s_xl2sb, g)
                if not isinstance(g, int) or g >= 2:
                    pe.wait_ge(s_x2, g - 1)
                for k in range(KH):
                    pe.matmul(pY[:, 0:C2], h1_hi[p][:, k, :], w2_hi[:, k, :], start=(k == 0), stop=False)
                    pe.matmul(pY[:, 0:C2], h1_hi[p][:, k, :], w2_lo[:, k, :], start=False, stop=False)
                    mm = pe.matmul(pY[:, 0:C2], h1_lo[p][:, k, :], w2_hi[:, k, :], start=False, stop=(k == KH - 1))
                mm.then_inc(s_xl2, 1)

            def transpose_scores2(g, p):
                pe.wait_ge(s_ab2, g + 1)
                pe.wait_ge(s_n0col, g + 1)
                if not isinstance(g, int) or g >= 2:
                    pe.wait_ge(s_h2lo, g - 1)
                if isinstance(g, int):
                    if min(g + 4, G) > 0:
                        pe.wait_ge(s_hTlo, min(g + 4, G))
                else:
                    pe.wait_ge(s_hTlo, g + 4)
                pe.transpose(pS[0:CW, 256:384], ab2[p][:, :].bitcast(F32), ident[:, :]).then_inc(s_R2, 1)

            def scores2(g, p):
                pe.wait_ge(s_rows2, g + 1)
                if isinstance(g, int):
                    pe.wait_ge(s_rows1, min(g + 4, G))
                else:
                    pe.wait_ge(s_rows1, g + 4)
                pe.matmul(pT[:, 256:384], of_graph(mask_all, g, N), ident_bf[:, :], start=True, stop=False)
                pe.matmul(pT[:, 256:384], rows2[p][:, :], sel_dst2[:, :], start=False, stop=False)
                pe.matmul(pT[:, 256:384], sel_src2[:, :], rows2[p][:, :], start=False, stop=True).then_inc(s_z2, 1)

            def transpose_P2(g, p):
                pe.wait_ge(s_P2, g + 1)
                if isinstance(g, int):
                    pe.wait_ge(s_L2, min(g + 1, G))
                else:
                    pe.wait_ge(s_L2, g + 1)
                pe.transpose(pT[:, 0:128], P2[p][:, :], ident[:, :]).then_inc(s_P2T, 1)

            def attend2(g, p):
                pe.wait_ge(s_PT2, g + 1)
                pe.wait_ge(s_xl2sb, min(g + 2, G) if isinstance(g, int) else g + 2)
                pe.matmul(pY[:, 0:D], PT2[p][:, :], xl2[p][:, :], start=True, stop=True).then_inc(s_attn2, 1)

            def transpose_h2(g, p):
                pe.wait_ge(s_h2n, g + 1)
                pe.wait_ge(s_hTlo, min(g + 6, G) if isinstance(g, int) else g + 6)
                pe.wait_ge(s_rows2, min(g + 2, G) if isinstance(g, int) else g + 2)
                for k in range(KD):
                    mm = pe.transpose(pS[:, k * 128:(k + 1) * 128], h2n[p][:, k * 128:(k + 1) * 128], ident[:, :])
                mm.then_inc(s_T2, 1)

            def convolve(g, p):
                pe.wait_ge(s_h2lo, g + 1)
                pe.wait_ge(s_L1, min(g + 5, G) if isinstance(g, int) else g + 5)
                for k in range(KD):
                    pe.matmul(pZ[:, 0:D], h2T_hi[p][:, k, :], w3_hi[:, k, :], start=(k == 0), stop=False)
                    pe.matmul(pZ[:, 0:D], h2T_hi[p][:, k, :], w3_lo[:, k, :], start=False, stop=False)
                    pe.matmul(pZ[:, 0:D], h2T_lo[p][:, k, :], w3_hi[:, k, :], start=False, stop=False)
                pe.matmul(pZ[:, 0:D], rows2[p][:, :], label_rows[:, :], start=False, stop=True).then_inc(s_fin, 1)

            pipeline(pe, [(project1, 0), (transpose_P2, 4), (convolve, 5), (transpose_scores1, 0), (transpose_P1, 1),
                          (transpose_scores2, 3), (attend2, 4), (scores1, 0), (attend1, 1), (transpose_h, -1),
                          (scores2, 3), (project2, 2), (transpose_h2, 4)])


_INS = ["x", "adj", "L0_gnn_W1", "L0_gnn_att_src1", "L0_gnn_att_dst1", "L0_gnn_b1", "L0_gnn_W2", "L0_gnn_att_src2",
        "L0_gnn_att_dst2", "L0_gnn_b2", "L1_gnn_weights", "L1_gnn_bias"]


def kernel(**inputs):
    import numpy as np
    import concourse.bacc as bacc
    from concourse.bass_utils import run_bass_kernel_spmd

    nc = bacc.Bacc("TRN2", target_bir_lowering=False, num_devices=1)
    arrays, args = {}, []
    for name in _INS:
        a = np.ascontiguousarray(inputs[name])
        arrays[f"in_{name}"] = a
        args.append(nc.dram_tensor(f"in_{name}", a.shape, mybir.dt.from_np(a.dtype), kind="ExternalInput").ap())
    args.append(nc.dram_tensor("out", inputs["x"].shape, mybir.dt.float32, kind="ExternalOutput").ap())
    gat_graphconv_block(nc, *args)
    r = run_bass_kernel_spmd(nc, [arrays], core_ids=[0])
    return r.results[0]["out"]
```

```python
import concourse.bass as bass
from concourse import mybir
from contextlib import ExitStack


def gat_graphconv_block(
    nc: bass.Bass,
    x: bass.AP,
    adj: bass.AP,
    W1: bass.AP,
    att_src1: bass.AP,
    att_dst1: bass.AP,
    b1: bass.AP,
    W2: bass.AP,
    att_src2: bass.AP,
    att_dst2: bass.AP,
    b2: bass.AP,
    W3: bass.AP,
    label_bias: bass.AP,
    out: bass.AP,
):
    F32 = mybir.dt.float32
    F32R = mybir.dt.float32r
    BF16 = mybir.dt.bfloat16
    I32 = mybir.dt.int32
    ALU = mybir.AluOpType
    ACT = mybir.ActivationFunctionType
    AX = mybir.AxisListType

    G, N, D = x.shape
    H, FH = att_src1.shape
    HF = H * FH
    KD = D // 128
    KH = HF // 128
    HALF = HF // 2
    C1 = HALF + 4
    C2 = D + 2
    SLOPE = 0.2
    EPS = 1e-5
    NEG = -float(2 ** 32)
    LO = 32
    RW = LO + 8
    CW = 72
    TURN = 4
    AHEAD = 8

    x_v = x.rearrange("g n c -> n g c")
    out_v = out.rearrange("g n c -> n g c")
    adj_v = adj.rearrange("g s d -> s g d")

    def row_of(h):
        return 4 * (h // 2) + h % 2

    def pipeline(eng, steps):
        lags = [lag for _, lag in steps]
        lo = -(-(max(lags) + 2) // TURN) * TURN
        hi = (G + min(lags)) // TURN * TURN

        def slot(t, place):
            for stage, lag in steps:
                g = t - lag
                if not isinstance(g, int) or 0 <= g < G:
                    stage(g, (place - lag) % TURN)

        for t in range(min(lags), lo):
            slot(t, t % TURN)
        with eng.Fori(lo // TURN, hi // TURN) as turn:
            for place in range(TURN):
                slot(TURN * turn + place, place)
        for t in range(hi, G + max(lags)):
            slot(t, t % TURN)

    def after(g, n):
        return not isinstance(g, int) or g >= n

    def upto(g, n):
        return min(g + n, G) if isinstance(g, int) else g + n

    with ExitStack() as ctx:
        def sb(name, shape, dt=F32):
            return ctx.enter_context(nc.sbuf_tensor(name, shape, dt))

        def pb(name, shape):
            return ctx.enter_context(nc.psum_tensor(name, shape, F32))

        def sem(name):
            return ctx.enter_context(nc.semaphore(name))

        def two(name, shape, dt=F32):
            return 2 * [sb(f"{name}{p}", shape, dt) for p in range(2)]

        x_all = sb("x_all", [128, G * D])
        adj_all = sb("adj_all", [128, G * N], I32)
        mask_all = sb("mask_all", [128, G * N], BF16)
        n0_all = sb("n0_all", [128, G])
        w1_hi = sb("w1_hi", [128, KD, 2, C1], F32R)
        w1_lo = sb("w1_lo", [128, KD, 2, C1], F32R)
        w2_hi = sb("w2_hi", [128, KH, C2], F32R)
        w2_lo = sb("w2_lo", [128, KH, C2], F32R)
        w3_hi = sb("w3_hi", [128, KD, D], F32R)
        w3_lo = sb("w3_lo", [128, KD, D], F32R)
        b1_bc = sb("b1_bc", [128, HF])
        b2_bc = sb("b2_bc", [128, D])
        ident = sb("ident", [128, 128])
        ident_bf = sb("ident_bf", [128, 128], BF16)
        off_diag = sb("off_diag", [128, 128], BF16)
        sel_src1 = sb("sel_src1", [RW, H, 128], F32R)
        sel_dst1 = sb("sel_dst1", [RW, H, 128], F32R)
        sel_src2 = sb("sel_src2", [RW, 128], F32R)
        sel_dst2 = sb("sel_dst2", [RW, 128], F32R)
        label_rows = sb("label_rows", [RW, D], F32R)
        minus_half = sb("minus_half", [128, 2])
        eps_col = sb("eps_col", [128, 2])

        staged = [G * D]

        def stage(*shape):
            size = 1
            for n in shape:
                size *= n
            staged[0] -= size
            names = "abc"[:len(shape)]
            return x_all[:, staged[0]:staged[0] + size].rearrange(
                f"p ({' '.join(names)}) -> p {' '.join(names)}", **dict(zip(names, shape)))

        w1_f = stage(KD, HF)
        w2_f = stage(KH, D)
        w3_f = stage(2, KD * D).rearrange("p j (k i) -> p j k i", k=KD)
        w1_cat = stage(KD, 2 * C1).rearrange("p k (a n) -> p k a n", a=2)
        w2_cat = stage(KH, C2)
        att1_bc = stage(2, HF)
        att2_bc = stage(2, D)
        w_att = stage(1, HF)[:, 0, :]
        lab = stage(2, D)[0:1]
        lab_f = stage(2, D)[0:1]
        assert staged[0] >= (AHEAD + 2) * 2 * D
        fold = sb("fold", [RW, 8])
        lab_parts = sb("lab_parts", [1, 4, D], F32R)

        hn = two("hn", [128, D])
        hT_hi = two("hT_hi", [128, KD, 128], F32R)
        hT_f = two("hT_f", [128, KD, 128])
        hT_lo = two("hT_lo", [128, KD, 128], F32R)
        xl = two("xl", [128, HF])
        ab1 = two("ab1", [128, CW], F32R)
        rows1 = two("rows1", [RW, 128], F32R)
        L1 = two("L1", [128, H, 128])
        nmax1 = two("nmax1", [128, H])
        sum1 = two("sum1", [128, H])
        rsum1 = two("rsum1", [128, H])
        P1 = two("P1", [128, H, 128])
        PT1 = two("PT1", [128, H, 128])
        elu_e = two("elu_e", [128, HF])
        h1 = two("h1", [128, HF])
        h1_hi = two("h1_hi", [128, KH, 128], F32R)
        h1_lo = two("h1_lo", [128, KH, 128], F32R)
        ab2 = two("ab2", [128, CW], F32R)
        xl2 = two("xl2", [128, D])
        rows2 = [sb(f"rows2_{p}", [RW, 128], F32R) for p in range(TURN)]
        L2 = two("L2", [128, 128])
        nmax2 = two("nmax2", [128, 1])
        sum2 = two("sum2", [128, 1])
        rsum2 = two("rsum2", [128, 1])
        P2 = two("P2", [128, 128])
        PT2 = two("PT2", [128, 128])
        h2n = two("h2n", [128, D])
        h2T_hi = two("h2T_hi", [128, KD, 128], F32R)
        h2T_f = two("h2T_f", [128, KD, 128])
        h2T_lo = two("h2T_lo", [128, KD, 128], F32R)
        bn1 = sb("bn1", [128, 2, 6])
        mv1 = sb("mv1", [128, 2, 2])
        ve1 = sb("ve1", [128, 2])
        rstd1 = sb("rstd1", [128, 2])
        bn2 = sb("bn2", [128, 6])
        mv2 = two("mv2", [128, 2])
        ve2 = sb("ve2", [128, 1])
        rstd2 = sb("rstd2", [128, 1])

        pX = pb("pX", [128, 2, 512])
        pZ = pb("pZ", [128, 512])
        pP = pb("pP", [128, H, 128])
        pA = pb("pA", [128, 512])
        pY = pb("pY", [128, 512])
        pS = pb("pS", [128, 512])
        pT = pb("pT", [128, 512])
        s_L1, s_L2 = sem("leaky1"), sem("leaky2")
        s_xdma, s_adjdma = sem("x_dma"), sem("adj_dma")
        s_loaded = sem("loaded")
        s_w1dma, s_w2dma, s_w3dma, s_labdma, s_labrow = (sem(n) for n in ("w1dma", "w2dma", "w3dma", "labdma", "labrow"))
        s_ident, s_consts, s_prep, s_w3T, s_w3ready, s_w1ready, s_w2ready = (
            sem(n) for n in ("ident", "consts", "prep", "w3T", "w3ready", "w1ready", "w2ready"))
        s_bn1, s_mv1, s_rs1a, s_rs1, s_hn = (sem(n) for n in ("bn1_done", "mv1_done", "rs1a", "rs1", "hn_done"))
        s_n0, s_mask, s_xb = sem("n0_done"), sem("mask_done"), sem("x_biased")
        s_T0, s_hThi, s_hTlo = sem("T0"), sem("hThi"), sem("hTlo")
        s_xl1, s_ab1hi, s_ab1, s_xlsb = sem("xl1"), sem("ab1hi"), sem("ab1_done"), sem("xl_sb")
        s_R1, s_rows1, s_z1, s_sc1, s_max1, s_exp1, s_rsum1, s_P1 = (
            sem(n) for n in ("R1", "rows1_sb", "z1", "scaled1", "max1", "exp1", "rsum1_done", "P1_done"))
        s_PT, s_PT1, s_attn1, s_E, s_elu_a, s_h1, s_h1hi, s_h1lo = (
            sem(n) for n in ("PT", "PT1_sb", "attn1", "elu_exp", "elu_a", "h1_done", "h1hi", "h1lo"))
        s_xl2, s_ab2hi, s_n0col, s_ab2, s_xl2sb = sem("xl2"), sem("ab2hi"), sem("n0col"), sem("ab2_done"), sem("xl2_sb")
        s_R2, s_rows2, s_z2, s_sc2, s_max2, s_exp2, s_rsum2, s_P2 = (
            sem(n) for n in ("R2", "rows2_sb", "z2", "scaled2", "max2", "exp2", "rsum2_done", "P2_done"))
        s_P2T, s_PT2, s_attn2, s_x2, s_bn2, s_mv2, s_rs2a, s_rs2, s_h2n = (
            sem(n) for n in ("P2T", "PT2_sb", "attn2", "x2", "bn2_done", "mv2_done", "rs2a", "rs2", "h2n_done"))
        s_T2, s_h2hi, s_h2lo, s_fin, s_out, s_stored = (
            sem(n) for n in ("T2", "h2hi", "h2lo", "final", "out_done", "stored"))

        block = ctx.enter_context(nc.Block())

        def of_graph(tile, g, width, graphs=1):
            return tile[:, bass.ds(g * width, graphs * width)]

        @block.sync
        def _(sp):
            def load(g, p):
                if p % 2:
                    return
                sp.dma_start(of_graph(x_all, g, D, 2).rearrange("n (g c) -> n g c", g=2),
                             x_v[:, bass.ds(g, 2), :]).then_inc(s_xdma, 16)
                sp.dma_start(of_graph(adj_all, g, N, 2).rearrange("n (g c) -> n g c", g=2),
                             adj_v[:, bass.ds(g, 2), :]).then_inc(s_adjdma, 16)
                sp.wait_ge(s_xdma, 8 * g + 16)
                sp.wait_ge(s_adjdma, 8 * g + 16)
                sp.sem_inc(s_loaded, 2)

            def store(g, p):
                if p % 2 == 0:
                    return
                sp.wait_ge(s_out, g + 1)
                sp.dma_start(out_v[:, bass.ds(g - 1, 2), :],
                             of_graph(x_all, g - 1, D, 2).rearrange("n (g c) -> n g c", g=2)).then_inc(s_stored, 16)

            pipeline(sp, [(load, -AHEAD), (store, 7)])
            sp.wait_ge(s_stored, 16 * (G // 2))

        @block.gpsimd
        def _(pool):
            pool.memset(ident[:, :], 0.0).then_inc(s_ident, 1)
            pool.memset(off_diag[:, :], NEG).then_inc(s_ident, 1)
            pool.memset(minus_half[:, :], -0.5).then_inc(s_ident, 1)
            pool.memset(eps_col[:, :], EPS).then_inc(s_ident, 1)
            pool.wait_ge(s_ident, 4)
            pool.affine_select(out=ident[:, :], in_=ident[:, :], compare_op=ALU.not_equal, fill=1.0,
                               base=0, pattern=[[-1, 128]], channel_multiplier=1).then_inc(s_ident, 1)
            pool.affine_select(out=off_diag[:, :], in_=off_diag[:, :], compare_op=ALU.not_equal, fill=0.0,
                               base=0, pattern=[[-1, 128]], channel_multiplier=1).then_inc(s_ident, 1)

            def inverse_std1(g, p):
                if p % 2:
                    return
                pool.wait_ge(s_mv1, g + 2)
                pool.tensor_tensor(ve1[:, :], mv1[:, :, 1], eps_col[:, :], ALU.add).then_inc(s_rs1a, 2)
                pool.wait_ge(s_rs1a, g + 2)
                pool.tensor_tensor(rstd1[:, :], ve1[:, :], minus_half[:, :], ALU.pow).then_inc(s_rs1, 2)

            def split_h1(g, p):
                pool.wait_ge(s_h1hi, g + 1)
                pool.tensor_tensor(h1_lo[p][:, :, :].rearrange("p a b -> p (a b)"), h1[p][:, :],
                                   h1_hi[p][:, :, :].rearrange("p a b -> p (a b)").bitcast(F32),
                                   ALU.subtract).then_inc(s_h1lo, 1)

            def inverse_std2(g, p):
                pool.wait_ge(s_mv2, g + 1)
                if after(g, 1):
                    pool.wait_ge(s_h2n, g)
                pool.tensor_tensor(ve2[:, :], mv2[p][:, 1:2], eps_col[:, 0:1], ALU.add).then_inc(s_rs2a, 1)
                pool.wait_ge(s_rs2a, g + 1)
                pool.tensor_tensor(rstd2[:, :], ve2[:, :], minus_half[:, 0:1], ALU.pow).then_inc(s_rs2, 1)

            def normalise1(g, p):
                pool.wait_ge(s_rsum1, g + 1)
                if after(g, 2):
                    pool.wait_ge(s_PT, g - 1)
                pool.tensor_tensor(P1[p][:, :, :], L1[p][:, :, :],
                                   rsum1[p][:, :].unsqueeze(2).broadcast_to([128, H, 128]), ALU.mult).then_inc(s_P1, 1)

            def low_h(g, p):
                pool.wait_ge(s_hThi, g + 1)
                if after(g, 2):
                    pool.wait_ge(s_xl1, g - 1)
                pool.tensor_tensor(hT_lo[p][:, :, :], hT_f[p][:, :, :], hT_hi[p][:, :, :].bitcast(F32),
                                   ALU.subtract).then_inc(s_hTlo, 1)

            def low_h2(g, p):
                pool.wait_ge(s_h2hi, g + 1)
                if after(g, 2):
                    pool.wait_ge(s_fin, g - 1)
                pool.tensor_tensor(h2T_lo[p][:, :, :], h2T_f[p][:, :, :], h2T_hi[p][:, :, :].bitcast(F32),
                                   ALU.subtract).then_inc(s_h2lo, 1)

            def mask_off_diagonal(g, p):
                if p % 2:
                    return
                pool.wait_ge(s_ident, 6)
                pool.wait_ge(s_n0, g + 2)
                pair = of_graph(mask_all, g, N, 2).rearrange("p (g d) -> p g d", g=2)
                pool.tensor_tensor(pair, pair, off_diag[:, :].unsqueeze(1).broadcast_to([128, 2, 128]),
                                   ALU.mult).then_inc(s_mask, 2)

            def add_bias2(g, p):
                pool.wait_ge(s_ident, 6)
                pool.wait_ge(s_hn, g + 1)
                pool.tensor_tensor(of_graph(x_all, g, D), of_graph(x_all, g, D), b2_bc[:, :], ALU.add).then_inc(s_xb, 1)

            pool.wait_ge(s_w2dma, 64)
            pipeline(pool, [(normalise1, 1), (split_h1, 2), (low_h2, 5), (inverse_std2, 4), (low_h, -1),
                            (add_bias2, -1), (mask_off_diagonal, -3), (inverse_std1, -3)])

        @block.scalar
        def _(act):
            act.dma_start(w1_f[:, :, :], W1.rearrange("(k p) n -> p k n", p=128)).then_inc(s_w1dma, 16)
            for j, a in enumerate((att_src1, att_dst1)):
                act.dma_start(att1_bc[:, j, :], a.rearrange("h f -> (h f)").unsqueeze(0).broadcast_to([128, HF])).then_inc(s_w1dma, 16)
            act.dma_start(b1_bc[:, :], b1.unsqueeze(0).broadcast_to([128, HF])).then_inc(s_w1dma, 16)
            act.dma_start(w2_f[:, :, :], W2.rearrange("(k p) n -> p k n", p=128)).then_inc(s_w2dma, 16)
            for j, a in enumerate((att_src2, att_dst2)):
                act.dma_start(att2_bc[:, j, :], a.broadcast_to([128, D])).then_inc(s_w2dma, 16)
            act.dma_start(b2_bc[:, :], b2.unsqueeze(0).broadcast_to([128, D])).then_inc(s_w2dma, 16)
            for j in range(2):
                act.dma_start(w3_f[:, j, :, :], W3[j].rearrange("(k o) i -> o k i", o=128)).then_inc(s_w3dma, 16)
            act.dma_start(lab[:, :, :], label_bias[0:2, :].unsqueeze(0)).then_inc(s_labdma, 16)

            def place_label_rows(g, p):
                if not isinstance(g, int) or g:
                    return
                act.wait_ge(s_consts, 1)
                act.wait_ge(s_w3ready, 2)
                for j in range(2):
                    act.dma_start(label_rows[LO * j + 2:LO * j + 4, :].bitcast(F32),
                                  lab_parts[:, 2 * j:2 * j + 2, :].bitcast(F32)).then_inc(s_labrow, 16)

            def no_edges(g, p):
                act.wait_ge(s_labdma, 16)
                act.wait_ge(s_loaded, g + 1)
                act.activation(of_graph(mask_all, g, N), of_graph(adj_all, g, N), ACT.Relu, bias=1.0, scale=-1.0,
                               accum_out=of_graph(n0_all, g, 1)).then_inc(s_n0, 1)

            def relu_h(g, p):
                act.wait_ge(s_T0, g + 1)
                if after(g, 2):
                    act.wait_ge(s_hTlo, g - 1)
                    act.wait_ge(s_xl1, g - 1)
                psum = pS[:, 0:D].rearrange("p (k n) -> p k n", k=KD)
                act.activation(hT_f[p][:, :, :], psum, ACT.Relu)
                act.activation(hT_hi[p][:, :, :], psum, ACT.Relu).then_inc(s_hThi, 1)

            def score_rows1(g, p):
                act.wait_ge(s_R1, g + 1)
                act.activation(rows1[p][:, :], pT[0:RW, 128:256], ACT.Copy).then_inc(s_rows1, 1)

            def scaled1(g, p):
                act.wait_ge(s_z1, g + 1)
                if after(g, 2):
                    act.wait_ge(s_P1, g - 1)
                act.activation(L1[p][:, :, :].rearrange("p h s -> p (h s)"), pZ[:, :], ACT.Copy, scale=SLOPE).then_inc(s_sc1, 1)

            def exp1(g, p):
                act.wait_ge(s_max1, g + 1)
                for h in range(H):
                    last = act.activation(L1[p][:, h, :], L1[p][:, h, :], ACT.Exp, bias=nmax1[p][:, h:h + 1],
                                          accum_out=sum1[p][:, h:h + 1])
                last.then_inc(s_exp1, 1)

            def copy_PT1(g, p):
                act.wait_ge(s_PT, g + 1)
                if after(g, 2):
                    act.wait_ge(s_attn1, g - 1)
                act.activation(PT1[p][:, :, :], pP[:, :, :], ACT.Copy).then_inc(s_PT1, 1)

            def elu_exp(g, p):
                act.wait_ge(s_attn1, g + 1)
                if after(g, 2):
                    act.wait_ge(s_h1, g - 1)
                act.activation(elu_e[p][:, :], pA[:, :], ACT.Exp).then_inc(s_E, 1)

            def score_rows2(g, p):
                act.wait_ge(s_R2, g + 1)
                if after(g, 4):
                    act.wait_ge(s_fin, g - 3)
                act.activation(rows2[p][:, :], pT[0:RW, 256:384], ACT.Copy).then_inc(s_rows2, 1)

            def scaled2(g, p):
                act.wait_ge(s_z2, g + 1)
                if after(g, 2):
                    act.wait_ge(s_P2, g - 1)
                act.activation(L2[p][:, :], pT[:, 384:512], ACT.Copy, scale=SLOPE).then_inc(s_sc2, 1)

            def exp2(g, p):
                act.wait_ge(s_max2, g + 1)
                act.activation(L2[p][:, :], L2[p][:, :], ACT.Exp, bias=nmax2[p][:, :],
                               accum_out=sum2[p][:, :]).then_inc(s_exp2, 1)

            def copy_PT2(g, p):
                act.wait_ge(s_P2T, g + 1)
                if after(g, 2):
                    act.wait_ge(s_attn2, g - 1)
                act.activation(PT2[p][:, :], pS[:, 256:384], ACT.Copy).then_inc(s_PT2, 1)

            def relu_h2(g, p):
                act.wait_ge(s_T2, g + 1)
                if after(g, 2):
                    act.wait_ge(s_h2lo, g - 1)
                    act.wait_ge(s_fin, g - 1)
                psum = pS[:, 0:D].rearrange("p (k n) -> p k n", k=KD)
                act.activation(h2T_f[p][:, :, :], psum, ACT.Relu)
                act.activation(h2T_hi[p][:, :, :], psum, ACT.Relu).then_inc(s_h2hi, 1)

            def high_h1(g, p):
                act.wait_ge(s_h1, g + 1)
                if after(g, 2):
                    act.wait_ge(s_xl2, g - 1)
                act.activation(h1_hi[p][:, :, :].rearrange("p a b -> p (a b)"), h1[p][:, :], ACT.Copy).then_inc(s_h1hi, 1)

            def features2(g, p):
                act.wait_ge(s_ab2, g + 1)
                if after(g, 2):
                    act.wait_ge(s_attn2, g - 1)
                act.activation(xl2[p][:, :], pY[:, 0:D], ACT.Copy).then_inc(s_xl2sb, 1)

            pipeline(act, [(features2, 3), (relu_h2, 5), (high_h1, 2), (place_label_rows, 4), (score_rows1, 0),
                           (copy_PT2, 4), (copy_PT1, 1), (score_rows2, 3), (no_edges, -4), (scaled1, 0), (scaled2, 3),
                           (relu_h, -1), (elu_exp, 1), (exp1, 0), (exp2, 3)])

        @block.vector
        def _(dve):
            prep = [0]

            def link(ins):
                prep[0] += 1
                ins.then_inc(s_prep, 1)
                dve.wait_ge(s_prep, prep[0])

            for p in range(2):
                dve.memset(ab1[p][:, :].bitcast(F32), 0.0)
                dve.memset(ab2[p][:, :].bitcast(F32), 0.0)
            dve.memset(label_rows[:, :].bitcast(F32), 0.0).then_inc(s_consts, 1)
            dve.wait_ge(s_ident, 6)
            link(dve.tensor_copy(ident_bf[:, :], ident[:, :]))
            link(dve.tensor_tensor(fold[:, :], ident[0:RW, 0:8], ident[0:RW, LO:LO + 8], ALU.add))
            for h in range(H):
                r = row_of(h)
                dve.tensor_copy(sel_src1[:, h, :], fold[:, r:r + 1].broadcast_to([RW, 128]))
                link(dve.tensor_copy(sel_dst1[:, h, :], fold[:, r + 2:r + 3].broadcast_to([RW, 128])))
            dve.tensor_copy(sel_src2[:, :], fold[:, 0:1].broadcast_to([RW, 128]))
            link(dve.tensor_copy(sel_dst2[:, :], fold[:, 1:2].broadcast_to([RW, 128])))
            for p in range(2):
                link(dve.memset(ab2[p][:, 3:RW:LO].bitcast(F32), 1.0))
            dve.tensor_copy(ident_bf[:, 0:1], ident[:, 0:1]).then_inc(s_consts, 1)

            def prepare_w1(g, p):
                if not isinstance(g, int) or g:
                    return
                dve.wait_ge(s_w1dma, 64)
                for k in range(KD):
                    for j in range(2):
                        link(dve.tensor_tensor(w_att[:, :], w1_f[:, k, :], att1_bc[:, j, :], ALU.mult))
                        link(dve.tensor_reduce(w1_cat[:, k, :, HALF + 2 * j:HALF + 2 * j + 2],
                                               w_att[:, :].rearrange("p (a h f) -> p a h f", a=2, h=2), AX.X, ALU.add))
                for k in range(KD):
                    link(dve.tensor_copy(w1_cat[:, k, :, 0:HALF], w1_f[:, k, :].rearrange("p (a n) -> p a n", a=2)))
                    link(dve.tensor_copy(w1_hi[:, k, :, :], w1_cat[:, k, :, :]))
                    link(dve.tensor_tensor(w1_lo[:, k, :, :], w1_cat[:, k, :, :], w1_hi[:, k, :, :].bitcast(F32), ALU.subtract))
                dve.tensor_copy(ident_bf[:, 0:1], ident[:, 0:1]).then_inc(s_w1ready, 1)

            def prepare_w2(g, p):
                if not isinstance(g, int) or g:
                    return
                dve.wait_ge(s_w2dma, 64)
                for k in range(KH):
                    for j in range(2):
                        link(dve.tensor_tensor(w_att[:, 0:D], w2_f[:, k, :], att2_bc[:, j, :], ALU.mult))
                        link(dve.tensor_reduce(w2_cat[:, k, D + j:D + j + 1], w_att[:, 0:D], AX.X, ALU.add))
                link(dve.tensor_copy(w2_cat[:, :, 0:D], w2_f[:, :, :]))
                link(dve.tensor_copy(w2_hi[:, :, :], w2_cat[:, :, :]))
                link(dve.tensor_tensor(w2_lo[:, :, :], w2_cat[:, :, :], w2_hi[:, :, :].bitcast(F32), ALU.subtract))
                dve.tensor_copy(ident_bf[:, 0:1], ident[:, 0:1]).then_inc(s_w2ready, 1)

            def prepare_w3(g, p):
                if not isinstance(g, int) or g:
                    return
                dve.wait_ge(s_w3dma, 32)
                link(dve.tensor_tensor(w3_f[:, 0, :, :], w3_f[:, 0, :, :], w3_f[:, 1, :, :], ALU.add))
                for k in range(KD):
                    link(dve.tensor_tensor(w3_f[:, 0, k, k * 128:(k + 1) * 128], w3_f[:, 0, k, k * 128:(k + 1) * 128],
                                           ident[:, :], ALU.add))
                dve.tensor_copy(ident_bf[:, 0:1], ident[:, 0:1]).then_inc(s_w3ready, 1)
                dve.wait_ge(s_labdma, 16)
                link(dve.tensor_tensor(lab_f[:, 0, :], lab[:, 0, :], lab[:, 1, :], ALU.subtract))
                link(dve.tensor_scalar(lab_f[:, 1, :], lab[:, 1, :], float(N), None, ALU.mult))
                link(dve.tensor_copy(lab_parts[:, 0:2, :], lab_f[:, :, :]))
                dve.tensor_tensor(lab_parts[:, 2:4, :], lab_f[:, :, :], lab_parts[:, 0:2, :].bitcast(F32),
                                  ALU.subtract).then_inc(s_w3ready, 1)

            def split_w3(g, p):
                if not isinstance(g, int) or g:
                    return
                dve.wait_ge(s_w3T, 1)
                w3T = pZ[:, :].rearrange("p (k o) -> p k o", k=KD)
                link(dve.tensor_copy(w3_hi[:, :, :], w3T))
                dve.tensor_tensor(w3_lo[:, :, :], w3T, w3_hi[:, :, :].bitcast(F32), ALU.subtract).then_inc(s_w3ready, 1)

            def stats1(g, p):
                if p % 2:
                    return
                dve.wait_ge(s_ident, 6)
                dve.wait_ge(s_loaded, g + 2)
                for j in range(2):
                    dve.bn_stats(bn1[:, j, :], of_graph(x_all, g + j, D)).then_inc(s_bn1, 1)
                dve.wait_ge(s_ident, 6)
                dve.wait_ge(s_bn1, g + 2)
                if after(g, 2):
                    dve.wait_ge(s_hn, g)
                dve.bn_aggr(mv1[:, 0, :], bn1[:, 0, :])
                dve.bn_aggr(mv1[:, 1, :], bn1[:, 1, :]).then_inc(s_mv1, 2)

            def layer_norm1(g, p):
                dve.wait_ge(s_rs1, g + 1)
                if after(g, 2):
                    dve.wait_ge(s_T0, g - 1)
                dve.tensor_scalar(hn[p][:, :], of_graph(x_all, g, D), mv1[:, p % 2, 0:1], rstd1[:, p % 2:p % 2 + 1],
                                  ALU.subtract, ALU.mult).then_inc(s_hn, 1)

            def layer_norm2(g, p):
                dve.wait_ge(s_rs2, g + 1)
                if after(g, 2):
                    dve.wait_ge(s_T2, g - 1)
                dve.tensor_scalar(h2n[p][:, :], of_graph(x_all, g, D), mv2[p][:, 0:1], rstd2[:, :],
                                  ALU.subtract, ALU.mult).then_inc(s_h2n, 1)

            def high_scores1(g, p):
                dve.wait_ge(s_xl1, g + 1)
                dve.tensor_copy(ab1[p][:, 0:8].rearrange("p (a c) -> p a c", a=2), pX[:, :, HALF:C1]).then_inc(s_ab1hi, 1)

            def low_scores1(g, p):
                dve.wait_ge(s_ab1hi, g + 1)
                dve.tensor_tensor(ab1[p][:, LO:LO + 8].rearrange("p (a c) -> p a c", a=2), pX[:, :, HALF:C1],
                                  ab1[p][:, 0:8].rearrange("p (a c) -> p a c", a=2).bitcast(F32),
                                  ALU.subtract).then_inc(s_ab1, 1)

            def features1(g, p):
                if after(g, 2):
                    dve.wait_ge(s_attn1, g - 1)
                dve.tensor_tensor(xl[p][:, :].rearrange("p (a n) -> p a n", a=2), pX[:, :, 0:HALF],
                                  b1_bc[:, :].rearrange("p (a n) -> p a n", a=2), ALU.add).then_inc(s_xlsb, 1)

            def leaky1(g, p):
                dve.wait_ge(s_sc1, g + 1)
                dve.tensor_tensor(L1[p][:, :, :].rearrange("p h s -> p (h s)"), pZ[:, :],
                                  L1[p][:, :, :].rearrange("p h s -> p (h s)"), ALU.max).then_inc(s_L1, 1)

            def max1(g, p):
                dve.wait_ge(s_L1, g + 1)
                dve.tensor_reduce(nmax1[p][:, :], L1[p][:, :, :], AX.X, ALU.max, negate=True).then_inc(s_max1, 1)

            def recip1(g, p):
                dve.wait_ge(s_exp1, g + 1)
                dve.reciprocal(rsum1[p][:, :], sum1[p][:, :]).then_inc(s_rsum1, 1)

            def elu_clamp(g, p):
                dve.wait_ge(s_E, g + 1)
                dve.tensor_scalar(elu_e[p][:, :], elu_e[p][:, :], 1.0, -1.0, ALU.min, ALU.add).then_inc(s_elu_a, 1)

            def elu_max(g, p):
                dve.wait_ge(s_elu_a, g + 1)
                if after(g, 2):
                    dve.wait_ge(s_h1lo, g - 1)
                dve.tensor_tensor(h1[p][:, :], pA[:, :], elu_e[p][:, :], ALU.max).then_inc(s_h1, 1)

            def scores2(g, p):
                dve.wait_ge(s_xl2, g + 1)
                dve.tensor_copy(ab2[p][:, 0:2], pY[:, D:C2]).then_inc(s_ab2hi, 1)
                dve.tensor_copy(ab2[p][:, 2:RW:LO], of_graph(n0_all, g, 1).broadcast_to([128, 2])).then_inc(s_n0col, 1)
                dve.wait_ge(s_ab2hi, g + 1)
                dve.tensor_tensor(ab2[p][:, LO:LO + 2], pY[:, D:C2], ab2[p][:, 0:2].bitcast(F32),
                                  ALU.subtract).then_inc(s_ab2, 1)

            def leaky2(g, p):
                dve.wait_ge(s_sc2, g + 1)
                dve.tensor_tensor(L2[p][:, :], pT[:, 384:512], L2[p][:, :], ALU.max).then_inc(s_L2, 1)

            def max2(g, p):
                dve.wait_ge(s_L2, g + 1)
                dve.tensor_reduce(nmax2[p][:, :], L2[p][:, :], AX.X, ALU.max, negate=True).then_inc(s_max2, 1)

            def recip2(g, p):
                dve.wait_ge(s_exp2, g + 1)
                dve.reciprocal(rsum2[p][:, :], sum2[p][:, :]).then_inc(s_rsum2, 1)

            def normalise2(g, p):
                dve.wait_ge(s_rsum2, g + 1)
                if after(g, 2):
                    dve.wait_ge(s_P2T, g - 1)
                dve.tensor_scalar(P2[p][:, :], L2[p][:, :], rsum2[p][:, :], None, ALU.mult).then_inc(s_P2, 1)

            def residual1(g, p):
                dve.wait_ge(s_attn2, g + 1)
                dve.wait_ge(s_xb, g + 1)
                dve.tensor_tensor(of_graph(x_all, g, D), pY[:, 0:D], of_graph(x_all, g, D), ALU.add).then_inc(s_x2, 1)

            def stats2(g, p):
                dve.wait_ge(s_ident, 6)
                dve.wait_ge(s_x2, g + 1)
                dve.bn_stats(bn2[:, :], of_graph(x_all, g, D)).then_inc(s_bn2, 1)

            def aggregate2(g, p):
                dve.wait_ge(s_ident, 6)
                dve.wait_ge(s_bn2, g + 1)
                if after(g, 2):
                    dve.wait_ge(s_h2n, g - 1)
                dve.bn_aggr(mv2[p][:, :], bn2[:, :]).then_inc(s_mv2, 1)

            def residual2(g, p):
                dve.wait_ge(s_fin, g + 1)
                dve.wait_ge(s_h2n, g + 1)
                dve.tensor_tensor(of_graph(x_all, g, D), pZ[:, 0:D], of_graph(x_all, g, D), ALU.add).then_inc(s_out, 1)

            pipeline(dve, [(elu_clamp, 2), (recip1, 1), (recip2, 4), (elu_max, 2), (normalise2, 4), (prepare_w1, 0),
                           (high_scores1, 0), (low_scores1, 0), (features1, 0), (residual2, 6), (split_w3, 4),
                           (residual1, 4), (layer_norm1, -2), (stats2, 4), (leaky1, 0), (aggregate2, 4), (max1, 0),
                           (layer_norm2, 4), (leaky2, 3), (stats1, -3), (max2, 3), (prepare_w2, 0), (prepare_w3, 3),
                           (scores2, 2)])

        @block.tensor
        def _(pe):
            pe.wait_ge(s_consts, 2)

            def transpose_w3(g, p):
                if not isinstance(g, int) or g:
                    return
                pe.wait_ge(s_w3ready, 1)
                pe.wait_ge(s_L1, 4)
                for ki in range(KD):
                    for ko in range(KD):
                        mm = pe.transpose(pZ[:, ki * D + ko * 128:ki * D + (ko + 1) * 128],
                                          w3_f[:, 0, ko, ki * 128:(ki + 1) * 128], ident[:, :])
                mm.then_inc(s_w3T, 1)

            def transpose_h(g, p):
                pe.wait_ge(s_hn, g + 1)
                if after(g, 5):
                    pe.wait_ge(s_PT2, g - 4)
                if after(g, 1):
                    pe.wait_ge(s_hThi, g)
                for k in range(KD):
                    mm = pe.transpose(pS[:, k * 128:(k + 1) * 128], hn[p][:, k * 128:(k + 1) * 128], ident[:, :])
                mm.then_inc(s_T0, 1)

            def project1(g, p):
                if isinstance(g, int) and g == 0:
                    pe.wait_ge(s_w1ready, 1)
                pe.wait_ge(s_hTlo, g + 1)
                if after(g, 1):
                    pe.wait_ge(s_xlsb, g)
                for a in range(2):
                    for k in range(KD):
                        pe.matmul(pX[:, a, 0:C1], hT_hi[p][:, k, :], w1_hi[:, k, a, :], start=(k == 0), stop=False)
                        pe.matmul(pX[:, a, 0:C1], hT_hi[p][:, k, :], w1_lo[:, k, a, :], start=False, stop=False)
                        mm = pe.matmul(pX[:, a, 0:C1], hT_lo[p][:, k, :], w1_hi[:, k, a, :], start=False, stop=(k == KD - 1))
                mm.then_inc(s_xl1, 1)

            def transpose_scores1(g, p):
                pe.wait_ge(s_ab1, g + 1)
                if after(g, 4):
                    pe.wait_ge(s_L2, g - 3)
                pe.transpose(pT[0:CW, 128:256], ab1[p][:, :].bitcast(F32), ident[:, :]).then_inc(s_R1, 1)

            def scores1(g, p):
                pe.wait_ge(s_mask, g + 1)
                pe.wait_ge(s_rows1, g + 1)
                if after(g, 1):
                    pe.wait_ge(s_L1, g)
                if isinstance(g, int) and g == 4:
                    pe.wait_ge(s_w3ready, 3)
                if after(g, 6):
                    pe.wait_ge(s_out, g - 5)
                pe.matmul(pZ[:, :].rearrange("p (h s) -> p h s", h=H), of_graph(mask_all, g, N),
                          ident_bf[:, :].unsqueeze(1).broadcast_to([128, H, 128]), start=True, stop=False)
                pe.matmul(pZ[:, :], rows1[p][:, :], sel_dst1[:, :, :].rearrange("p h s -> p (h s)"), start=False, stop=False)
                for h in range(H):
                    mm = pe.matmul(pZ[:, h * 128:(h + 1) * 128], sel_src1[:, h, :], rows1[p][:, :], start=False, stop=(h == H - 1))
                mm.then_inc(s_z1, 1)

            def transpose_P1(g, p):
                pe.wait_ge(s_P1, g + 1)
                if after(g, 1):
                    pe.wait_ge(s_PT1, g)
                for h in range(H):
                    mm = pe.transpose(pP[:, h, :], P1[p][:, h, :], ident[:, :])
                mm.then_inc(s_PT, 1)

            def attend1(g, p):
                pe.wait_ge(s_PT1, g + 1)
                pe.wait_ge(s_xlsb, g + 1)
                if after(g, 1):
                    pe.wait_ge(s_h1, g)
                for h in range(H):
                    mm = pe.matmul(pA[:, h * 128:(h + 1) * 128], xl[p][:, h * FH:(h + 1) * FH], PT1[p][:, h, :],
                                   start=True, stop=True)
                mm.then_inc(s_attn1, 1)

            def project2(g, p):
                if isinstance(g, int) and g == 0:
                    pe.wait_ge(s_w2ready, 1)
                pe.wait_ge(s_h1lo, g + 1)
                if after(g, 1):
                    pe.wait_ge(s_xl2sb, g)
                if after(g, 2):
                    pe.wait_ge(s_x2, g - 1)
                for k in range(KH):
                    pe.matmul(pY[:, 0:C2], h1_hi[p][:, k, :], w2_hi[:, k, :], start=(k == 0), stop=False)
                    pe.matmul(pY[:, 0:C2], h1_hi[p][:, k, :], w2_lo[:, k, :], start=False, stop=False)
                    mm = pe.matmul(pY[:, 0:C2], h1_lo[p][:, k, :], w2_hi[:, k, :], start=False, stop=(k == KH - 1))
                mm.then_inc(s_xl2, 1)

            def transpose_scores2(g, p):
                pe.wait_ge(s_ab2, g + 1)
                pe.wait_ge(s_n0col, g + 1)
                pe.wait_ge(s_rows1, upto(g, 4))
                pe.transpose(pT[0:CW, 256:384], ab2[p][:, :].bitcast(F32), ident[:, :]).then_inc(s_R2, 1)

            def scores2(g, p):
                pe.wait_ge(s_rows2, g + 1)
                z2 = pT[:, 384:512]
                pe.matmul(z2, of_graph(mask_all, g, N), ident_bf[:, :], start=True, stop=False)
                pe.matmul(z2, rows2[p][:, :], sel_dst2[:, :], start=False, stop=False)
                pe.matmul(z2, sel_src2[:, :], rows2[p][:, :], start=False, stop=True).then_inc(s_z2, 1)

            def transpose_P2(g, p):
                pe.wait_ge(s_P2, g + 1)
                if after(g, 1):
                    pe.wait_ge(s_h2hi, g)
                pe.transpose(pS[:, 256:384], P2[p][:, :], ident[:, :]).then_inc(s_P2T, 1)

            def attend2(g, p):
                pe.wait_ge(s_PT2, g + 1)
                pe.wait_ge(s_xl2sb, upto(g, 2))
                pe.matmul(pY[:, 0:D], PT2[p][:, :], xl2[p][:, :], start=True, stop=True).then_inc(s_attn2, 1)

            def transpose_h2(g, p):
                pe.wait_ge(s_h2n, g + 1)
                pe.wait_ge(s_hThi, upto(g, 6))
                for k in range(KD):
                    mm = pe.transpose(pS[:, k * 128:(k + 1) * 128], h2n[p][:, k * 128:(k + 1) * 128], ident[:, :])
                mm.then_inc(s_T2, 1)

            def convolve(g, p):
                pe.wait_ge(s_h2lo, g + 1)
                pe.wait_ge(s_L1, upto(g, 6))
                if after(g, 1):
                    pe.wait_ge(s_out, g)
                if isinstance(g, int) and g == 0:
                    pe.wait_ge(s_w3ready, 3)
                    pe.wait_ge(s_labrow, 32)
                for k in range(KD):
                    pe.matmul(pZ[:, 0:D], h2T_hi[p][:, k, :], w3_hi[:, k, :], start=(k == 0), stop=False)
                    pe.matmul(pZ[:, 0:D], h2T_hi[p][:, k, :], w3_lo[:, k, :], start=False, stop=False)
                    pe.matmul(pZ[:, 0:D], h2T_lo[p][:, k, :], w3_hi[:, k, :], start=False, stop=False)
                pe.matmul(pZ[:, 0:D], rows2[p][:, :], label_rows[:, :], start=False, stop=True).then_inc(s_fin, 1)

            pipeline(pe, [(project1, 0), (convolve, 6), (transpose_w3, 4), (transpose_scores1, 0), (transpose_P2, 4),
                          (transpose_P1, 1), (transpose_scores2, 3), (attend2, 4), (scores1, 0), (scores2, 3),
                          (transpose_h, -1), (attend1, 1), (project2, 2), (transpose_h2, 4)])


_INS = ["x", "adj", "L0_gnn_W1", "L0_gnn_att_src1", "L0_gnn_att_dst1", "L0_gnn_b1", "L0_gnn_W2", "L0_gnn_att_src2",
        "L0_gnn_att_dst2", "L0_gnn_b2", "L1_gnn_weights", "L1_gnn_bias"]


def kernel(**inputs):
    import numpy as np
    import concourse.bacc as bacc
    from concourse.bass_utils import run_bass_kernel_spmd

    nc = bacc.Bacc("TRN2", target_bir_lowering=False, num_devices=1)
    arrays, args = {}, []
    for name in _INS:
        a = np.ascontiguousarray(inputs[name])
        arrays[f"in_{name}"] = a
        args.append(nc.dram_tensor(f"in_{name}", a.shape, mybir.dt.from_np(a.dtype), kind="ExternalInput").ap())
    args.append(nc.dram_tensor("out", inputs["x"].shape, mybir.dt.float32, kind="ExternalOutput").ap())
    gat_graphconv_block(nc, *args)
    r = run_bass_kernel_spmd(nc, [arrays], core_ids=[0])
    return r.results[0]["out"]
```

```python
import concourse.bass as bass
from concourse import mybir
from contextlib import ExitStack


def gat_graphconv_block(
    nc: bass.Bass,
    x: bass.AP,
    adj: bass.AP,
    W1: bass.AP,
    att_src1: bass.AP,
    att_dst1: bass.AP,
    b1: bass.AP,
    W2: bass.AP,
    att_src2: bass.AP,
    att_dst2: bass.AP,
    b2: bass.AP,
    W3: bass.AP,
    label_bias: bass.AP,
    out: bass.AP,
):
    F32 = mybir.dt.float32
    F32R = mybir.dt.float32r
    BF16 = mybir.dt.bfloat16
    I32 = mybir.dt.int32
    ALU = mybir.AluOpType
    ACT = mybir.ActivationFunctionType
    AX = mybir.AxisListType

    G, N, D = x.shape
    LABELS = label_bias.shape[0]
    H, FH = att_src1.shape
    HF = H * FH
    KD = D // 128
    KH = HF // 128
    HALF = HF // 2
    C1 = HALF + 4
    C2 = D + 2
    SLOPE = 0.2
    EPS = 1e-5
    NEG = -float(2 ** 32)
    LO = 32
    RW = LO + 8
    CW = 72
    TURN = 4
    AHEAD = 8

    x_v = x.rearrange("g n c -> n g c")
    out_v = out.rearrange("g n c -> n g c")
    adj_v = adj.rearrange("g s d -> s g d")

    def row_of(h):
        return 4 * (h // 2) + h % 2

    def pipeline(eng, steps):
        lags = [lag for _, lag in steps]
        lo = -(-(max(lags) + 2) // TURN) * TURN
        hi = (G + min(lags)) // TURN * TURN

        def slot(t, place):
            for stage, lag in steps:
                g = t - lag
                if not isinstance(g, int) or 0 <= g < G:
                    stage(g, (place - lag) % TURN)

        for t in range(min(lags), lo):
            slot(t, t % TURN)
        with eng.Fori(lo // TURN, hi // TURN) as turn:
            for place in range(TURN):
                slot(TURN * turn + place, place)
        for t in range(hi, G + max(lags)):
            slot(t, t % TURN)

    def after(g, n):
        return not isinstance(g, int) or g >= n

    def alone(g, n=1):
        return isinstance(g, int) and g >= n

    def upto(g, n):
        return min(g + n, G) if isinstance(g, int) else g + n

    with ExitStack() as ctx:
        def sb(name, shape, dt=F32):
            return ctx.enter_context(nc.sbuf_tensor(name, shape, dt))

        def pb(name, shape):
            return ctx.enter_context(nc.psum_tensor(name, shape, F32))

        def sem(name):
            return ctx.enter_context(nc.semaphore(name))

        def two(name, shape, dt=F32):
            return 2 * [sb(f"{name}{p}", shape, dt) for p in range(2)]

        x_all = sb("x_all", [128, G * D])
        adj_all = sb("adj_all", [128, G * N], I32)
        mask_all = sb("mask_all", [128, G * N], BF16)
        n0_all = sb("n0_all", [128, G])
        w1_hi = sb("w1_hi", [128, KD, 2, C1], F32R)
        w1_lo = sb("w1_lo", [128, KD, 2, C1], F32R)
        w2_hi = sb("w2_hi", [128, KH, C2], F32R)
        w2_lo = sb("w2_lo", [128, KH, C2], F32R)
        w3_hi = sb("w3_hi", [128, KD, D], F32R)
        w3_lo = sb("w3_lo", [128, KD, D], F32R)
        b1_bc = sb("b1_bc", [128, HF])
        b2_bc = sb("b2_bc", [128, D])
        ident = sb("ident", [128, 128])
        ident_r = sb("ident_r", [128, 128], F32R)
        ident_bf = sb("ident_bf", [128, 128], BF16)
        off_diag = sb("off_diag", [128, 128], BF16)
        sel_src1 = sb("sel_src1", [RW, H, 128], F32R)
        sel_dst1 = sb("sel_dst1", [RW, H, 128], F32R)
        sel_src2 = sb("sel_src2", [RW, 128], F32R)
        sel_dst2 = sb("sel_dst2", [RW, 128], F32R)
        label_rows = sb("label_rows", [RW, D], F32R)
        minus_half = sb("minus_half", [128, 2])
        eps_col = sb("eps_col", [128, 2])

        staged = [G * D]

        def stage(*shape):
            size = 1
            for n in shape:
                size *= n
            staged[0] -= size
            names = "abc"[:len(shape)]
            return x_all[:, staged[0]:staged[0] + size].rearrange(
                f"p ({' '.join(names)}) -> p {' '.join(names)}", **dict(zip(names, shape)))

        w1_f = stage(KD, HF)
        w2_f = stage(KH, D)
        w3_f = stage(2, KD * D).rearrange("p j (k i) -> p j k i", k=KD)
        att1_bc = stage(2, HF)
        att2_bc = stage(2, D)
        w1_att = stage(2, KD * HF)
        w2_att = stage(2, KH * D)
        lab = stage(2, D)[0:1]
        lab_f = stage(2, D)[0:1]
        lab_parts = stage(4, D)[0:1].bitcast(F32R)
        assert staged[0] >= (AHEAD + 2) * 2 * D
        fold = sb("fold", [RW, 8])
        w1_scores = sb("w1_scores", [128, 2, KD * H])
        w2_scores = sb("w2_scores", [128, 2, KH])

        top_label = sb("top_label", [128, G // 2])
        top = sb("top", [128, 1])
        top_row = sb("top_row", [1, 1])
        top_int = sb("top_int", [1, 1], I32)
        assert LABELS * D <= G * N // 2
        bias_bc = mask_all[:, 0:2 * LABELS * D].bitcast(F32).rearrange("p (l c) -> p l c", l=LABELS)
        label_no = sb("label_no", [128, LABELS - 2])
        is_label = sb("is_label", [128, LABELS - 2, N], BF16)
        label_count = sb("label_count", [128, LABELS - 2])

        hn = two("hn", [128, D])
        hT_hi = two("hT_hi", [128, KD, 128], F32R)
        hT_f = two("hT_f", [128, KD, 128])
        hT_lo = two("hT_lo", [128, KD, 128], F32R)
        xl = two("xl", [128, HF])
        ab1 = two("ab1", [128, CW], F32R)
        rows1 = two("rows1", [RW, 128], F32R)
        L1 = two("L1", [128, H, 128])
        nmax1 = two("nmax1", [128, H])
        sum1 = two("sum1", [128, H])
        rsum1 = two("rsum1", [128, H])
        P1 = two("P1", [128, H, 128])
        PT1 = two("PT1", [128, H, 128])
        elu_e = two("elu_e", [128, HF])
        h1 = two("h1", [128, HF])
        h1_hi = two("h1_hi", [128, KH, 128], F32R)
        h1_lo = two("h1_lo", [128, KH, 128], F32R)
        ab2 = two("ab2", [128, CW], F32R)
        xl2 = two("xl2", [128, D])
        rows2 = [sb(f"rows2_{p}", [RW, 128], F32R) for p in range(TURN)]
        L2 = two("L2", [128, 128])
        nmax2 = two("nmax2", [128, 1])
        sum2 = two("sum2", [128, 1])
        rsum2 = two("rsum2", [128, 1])
        P2 = two("P2", [128, 128])
        PT2 = two("PT2", [128, 128])
        h2n = two("h2n", [128, D])
        h2T_hi = two("h2T_hi", [128, KD, 128], F32R)
        h2T_f = two("h2T_f", [128, KD, 128])
        h2T_lo = two("h2T_lo", [128, KD, 128], F32R)
        bn1 = sb("bn1", [128, 2, 6])
        mv1 = sb("mv1", [128, 2, 2])
        ve1 = sb("ve1", [128, 2])
        rstd1 = sb("rstd1", [128, 2])
        bn2 = sb("bn2", [128, 6])
        mv2 = two("mv2", [128, 2])
        ve2 = sb("ve2", [128, 1])
        rstd2 = sb("rstd2", [128, 1])

        pX = pb("pX", [128, 2, 512])
        pA = pb("pA", [128, 512])
        pF = pb("pF", [128, 512])
        pT = pb("pT", [128, 512])
        pH = pb("pH", [128, 512])
        pZ = pb("pZ", [128, 512])
        pS = pb("pS", [128, 512])
        s_L1, s_L2 = sem("leaky1"), sem("leaky2")
        s_xdma, s_adjdma = sem("x_dma"), sem("adj_dma")
        s_loaded = sem("loaded")
        s_w1dma, s_w2dma, s_w3dma, s_labdma, s_labrow = (sem(n) for n in ("w1dma", "w2dma", "w3dma", "labdma", "labrow"))
        s_ident, s_consts, s_prep, s_w3T, s_w3ready, s_w1ready, s_w2ready = (
            sem(n) for n in ("ident", "consts", "prep", "w3T", "w3ready", "w1ready", "w2ready"))
        s_w1att, s_w2att, s_w1hi, s_w2hi, s_w2lo = (sem(n) for n in ("w1att", "w2att", "w1hi", "w2hi", "w2lo"))
        s_bn1, s_mv1, s_rs1a, s_rs1, s_hn = (sem(n) for n in ("bn1_done", "mv1_done", "rs1a", "rs1", "hn_done"))
        s_n0, s_mask, s_xb = sem("n0_done"), sem("mask_done"), sem("x_biased")
        s_T0, s_hThi, s_hTlo = sem("T0"), sem("hThi"), sem("hTlo")
        s_xl1, s_ab1hi, s_ab1, s_xlsb = sem("xl1"), sem("ab1hi"), sem("ab1_done"), sem("xl_sb")
        s_R1, s_rows1, s_z1, s_sc1, s_max1, s_exp1, s_rsum1, s_P1 = (
            sem(n) for n in ("R1", "rows1_sb", "z1", "scaled1", "max1", "exp1", "rsum1_done", "P1_done"))
        s_PT, s_PT1, s_attn1, s_E, s_elu_a, s_h1, s_h1hi, s_h1lo = (
            sem(n) for n in ("PT", "PT1_sb", "attn1", "elu_exp", "elu_a", "h1_done", "h1hi", "h1lo"))
        s_xl2, s_ab2hi, s_n0col, s_ab2, s_xl2sb = sem("xl2"), sem("ab2hi"), sem("n0col"), sem("ab2_done"), sem("xl2_sb")
        s_R2, s_rows2, s_z2, s_sc2, s_max2, s_exp2, s_rsum2, s_P2 = (
            sem(n) for n in ("R2", "rows2_sb", "z2", "scaled2", "max2", "exp2", "rsum2_done", "P2_done"))
        s_P2T, s_PT2, s_attn2, s_x2, s_bn2, s_mv2, s_rs2a, s_rs2, s_h2n = (
            sem(n) for n in ("P2T", "PT2_sb", "attn2", "x2", "bn2_done", "mv2_done", "rs2a", "rs2", "h2n_done"))
        s_T2, s_h2hi, s_h2lo, s_fin, s_out, s_stored = (
            sem(n) for n in ("T2", "h2hi", "h2lo", "final", "out_done", "stored"))

        s_top, s_toprow, s_label, s_biasdma, s_diff, s_fixed, s_restored = (
            sem(n) for n in ("top", "top_row", "top_label_known", "bias_dma", "bias_diff", "fixed", "restored"))

        block = ctx.enter_context(nc.Block())
        FIX = LABELS
        STORES = 16 * (G // 2)

        def of_graph(tile, g, width, graphs=1):
            return tile[:, bass.ds(g * width, graphs * width)]

        @block.sync
        def _(sp):
            def load(g, p):
                if p % 2:
                    return
                sp.dma_start(of_graph(x_all, g, D, 2).rearrange("n (g c) -> n g c", g=2),
                             x_v[:, bass.ds(g, 2), :]).then_inc(s_xdma, 16)
                sp.dma_start(of_graph(adj_all, g, N, 2).rearrange("n (g c) -> n g c", g=2),
                             adj_v[:, bass.ds(g, 2), :]).then_inc(s_adjdma, 16)
                sp.wait_ge(s_xdma, 8 * g + 16)
                sp.wait_ge(s_adjdma, 8 * g + 16)
                sp.sem_inc(s_loaded, 2)

            def load_late_weights(g, p):
                if not isinstance(g, int) or g:
                    return
                sp.dma_start(w2_f[:, :, :], W2.rearrange("(k p) n -> p k n", p=128)).then_inc(s_w2dma, 16)
                for j, a in enumerate((att_src2, att_dst2)):
                    sp.dma_start(att2_bc[:, j, :], a.broadcast_to([128, D])).then_inc(s_w2dma, 16)
                sp.dma_start(b2_bc[:, :], b2.unsqueeze(0).broadcast_to([128, D])).then_inc(s_w2dma, 16)
                for j in range(2):
                    sp.dma_start(w3_f[:, j, :, :], W3[j].rearrange("(k o) i -> o k i", o=128)).then_inc(s_w3dma, 16)
                sp.dma_start(lab[:, :, :], label_bias[0:2, :].unsqueeze(0)).then_inc(s_labdma, 16)

            def store(g, p):
                if p % 2 == 0:
                    return
                sp.wait_ge(s_out, g + 1)
                sp.dma_start(out_v[:, bass.ds(g - 1, 2), :],
                             of_graph(x_all, g - 1, D, 2).rearrange("n (g c) -> n g c", g=2)).then_inc(s_stored, 16)

            pipeline(sp, [(load, -AHEAD), (load_late_weights, -AHEAD + 2), (store, 7)])
            sp.wait_ge(s_label, 1)
            largest = sp.value_load(top_int[0:1, 0:1], min_val=0, max_val=LABELS - 1)
            sp.wait_ge(s_stored, STORES)
            with sp.If(largest > 1):
                sp.dma_start(bias_bc[:, :, :], label_bias.unsqueeze(0).broadcast_to([128, LABELS, D])).then_inc(s_biasdma, 16)
                with sp.Fori(0, G) as g:
                    sp.wait_ge(s_fixed, FIX * (g + 1))
                    sp.dma_start(out_v[:, bass.ds(g, 1), :],
                                 of_graph(x_all, g, D).rearrange("n (g c) -> n g c", g=1)).then_inc(s_restored, 16)
                sp.wait_ge(s_restored, 16 * G)

        @block.gpsimd
        def _(pool):
            pool.memset(ident[:, :], 0.0).then_inc(s_ident, 1)
            pool.memset(off_diag[:, :], NEG).then_inc(s_ident, 1)
            pool.memset(minus_half[:, :], -0.5).then_inc(s_ident, 1)
            pool.memset(eps_col[:, :], EPS).then_inc(s_ident, 1)
            pool.wait_ge(s_ident, 4)
            pool.affine_select(out=ident[:, :], in_=ident[:, :], compare_op=ALU.not_equal, fill=1.0,
                               base=0, pattern=[[-1, 128]], channel_multiplier=1).then_inc(s_ident, 1)
            pool.affine_select(out=off_diag[:, :], in_=off_diag[:, :], compare_op=ALU.not_equal, fill=0.0,
                               base=0, pattern=[[-1, 128]], channel_multiplier=1).then_inc(s_ident, 1)

            def inverse_std1(g, p):
                if p % 2:
                    return
                pool.wait_ge(s_mv1, g + 2)
                pool.tensor_tensor(ve1[:, :], mv1[:, :, 1], eps_col[:, :], ALU.add).then_inc(s_rs1a, 2)
                pool.wait_ge(s_rs1a, g + 2)
                pool.tensor_tensor(rstd1[:, :], ve1[:, :], minus_half[:, :], ALU.pow).then_inc(s_rs1, 2)

            def split_h1(g, p):
                pool.wait_ge(s_h1hi, g + 1)
                pool.tensor_tensor(h1_lo[p][:, :, :].rearrange("p a b -> p (a b)"), h1[p][:, :],
                                   h1_hi[p][:, :, :].rearrange("p a b -> p (a b)").bitcast(F32),
                                   ALU.subtract).then_inc(s_h1lo, 1)

            def inverse_std2(g, p):
                pool.wait_ge(s_mv2, g + 1)
                if after(g, 1):
                    pool.wait_ge(s_h2n, g)
                pool.tensor_tensor(ve2[:, :], mv2[p][:, 1:2], eps_col[:, 0:1], ALU.add).then_inc(s_rs2a, 1)
                pool.wait_ge(s_rs2a, g + 1)
                pool.tensor_tensor(rstd2[:, :], ve2[:, :], minus_half[:, 0:1], ALU.pow).then_inc(s_rs2, 1)

            def normalise1(g, p):
                pool.wait_ge(s_rsum1, g + 1)
                if after(g, 2):
                    pool.wait_ge(s_PT, g - 1)
                pool.tensor_tensor(P1[p][:, :, :], L1[p][:, :, :],
                                   rsum1[p][:, :].unsqueeze(2).broadcast_to([128, H, 128]), ALU.mult).then_inc(s_P1, 1)

            def low_h(g, p):
                pool.wait_ge(s_hThi, g + 1)
                if after(g, 2):
                    pool.wait_ge(s_xl1, g - 1)
                pool.tensor_tensor(hT_lo[p][:, :, :], hT_f[p][:, :, :], hT_hi[p][:, :, :].bitcast(F32),
                                   ALU.subtract).then_inc(s_hTlo, 1)

            def low_h2(g, p):
                pool.wait_ge(s_h2hi, g + 1)
                if after(g, 2):
                    pool.wait_ge(s_fin, g - 1)
                pool.tensor_tensor(h2T_lo[p][:, :, :], h2T_f[p][:, :, :], h2T_hi[p][:, :, :].bitcast(F32),
                                   ALU.subtract).then_inc(s_h2lo, 1)

            def mask_off_diagonal(g, p):
                if p % 2:
                    return
                pool.wait_ge(s_ident, 6)
                pool.wait_ge(s_n0, g + 2)
                pair = of_graph(mask_all, g, N, 2).rearrange("p (g d) -> p g d", g=2)
                pool.tensor_tensor(pair, pair, off_diag[:, :].unsqueeze(1).broadcast_to([128, 2, 128]),
                                   ALU.mult).then_inc(s_mask, 2)

            def add_bias2(g, p):
                if isinstance(g, int) and g == 0:
                    pool.wait_ge(s_w2dma, 64)
                pool.wait_ge(s_ident, 6)
                pool.wait_ge(s_hn, g + 1)
                pool.tensor_tensor(of_graph(x_all, g, D), of_graph(x_all, g, D), b2_bc[:, :], ALU.add).then_inc(s_xb, 1)

            def weigh_w1(g, p):
                if not isinstance(g, int) or g:
                    return
                pool.wait_ge(s_w1dma, 64)
                pool.tensor_tensor(w1_att[:, 1, :].rearrange("p (k n) -> p k n", k=KD), w1_f[:, :, :],
                                   att1_bc[:, 1, :].unsqueeze(1).broadcast_to([128, KD, HF]), ALU.mult).then_inc(s_w1att, 1)

            def weigh_w2(g, p):
                if not isinstance(g, int) or g:
                    return
                pool.wait_ge(s_w2dma, 64)
                pool.tensor_tensor(w2_att[:, 1, :].rearrange("p (k n) -> p k n", k=KH), w2_f[:, :, :],
                                   att2_bc[:, 1, :].unsqueeze(1).broadcast_to([128, KH, D]), ALU.mult).then_inc(s_w2att, 1)
                pool.wait_ge(s_w2hi, 1)
                pool.tensor_tensor(w2_lo[:, :, 0:D], w2_f[:, :, :], w2_hi[:, :, 0:D].bitcast(F32),
                                   ALU.subtract).then_inc(s_w2lo, 1)

            pipeline(pool, [(normalise1, 1), (inverse_std2, 5), (mask_off_diagonal, -2), (add_bias2, 4), (low_h, -1),
                            (weigh_w2, 0), (inverse_std1, -3), (weigh_w1, -3), (split_h1, 2), (low_h2, 5)])

        @block.scalar
        def _(act):
            act.dma_start(w1_f[:, :, :], W1.rearrange("(k p) n -> p k n", p=128)).then_inc(s_w1dma, 16)
            for j, a in enumerate((att_src1, att_dst1)):
                act.dma_start(att1_bc[:, j, :], a.rearrange("h f -> (h f)").unsqueeze(0).broadcast_to([128, HF])).then_inc(s_w1dma, 16)
            act.dma_start(b1_bc[:, :], b1.unsqueeze(0).broadcast_to([128, HF])).then_inc(s_w1dma, 16)

            def place_label_rows(g, p):
                if not isinstance(g, int) or g:
                    return
                act.wait_ge(s_consts, 1)
                act.wait_ge(s_w3ready, 2)
                for j in range(2):
                    act.dma_start(label_rows[LO * j + 2:LO * j + 4, :].bitcast(F32),
                                  lab_parts[:, 2 * j:2 * j + 2, :].bitcast(F32)).then_inc(s_labrow, 16)

            def no_edges(g, p):
                act.wait_ge(s_ident, 6)
                act.wait_ge(s_loaded, g + 1)
                act.activation(of_graph(mask_all, g, N), of_graph(adj_all, g, N), ACT.Relu, bias=1.0, scale=-1.0,
                               accum_out=of_graph(n0_all, g, 1)).then_inc(s_n0, 1)

            def relu_h(g, p):
                act.wait_ge(s_T0, g + 1)
                if after(g, 2):
                    act.wait_ge(s_hTlo, g - 1)
                    act.wait_ge(s_xl1, g - 1)
                psum = pS[:, 0:D].rearrange("p (k n) -> p k n", k=KD)
                act.activation(hT_f[p][:, :, :], psum, ACT.Relu)
                act.activation(hT_hi[p][:, :, :], psum, ACT.Relu).then_inc(s_hThi, 1)

            def score_rows1(g, p):
                act.wait_ge(s_R1, g + 1)
                act.activation(rows1[p][:, :], pT[0:RW, 128:256], ACT.Copy).then_inc(s_rows1, 1)

            def scaled1(g, p):
                act.wait_ge(s_z1, g + 1)
                if after(g, 2):
                    act.wait_ge(s_P1, g - 1)
                act.activation(L1[p][:, :, :].rearrange("p h s -> p (h s)"), pZ[:, :], ACT.Copy, scale=SLOPE).then_inc(s_sc1, 1)

            def exp1(g, p):
                act.wait_ge(s_max1, g + 1)
                for h in range(H):
                    last = act.activation(L1[p][:, h, :], L1[p][:, h, :], ACT.Exp, bias=nmax1[p][:, h:h + 1],
                                          accum_out=sum1[p][:, h:h + 1])
                last.then_inc(s_exp1, 1)

            def copy_PT1(g, p):
                act.wait_ge(s_PT, g + 1)
                if after(g, 2):
                    act.wait_ge(s_attn1, g - 1)
                act.activation(PT1[p][:, :, :].rearrange("p h s -> p (h s)"), pA[:, :], ACT.Copy).then_inc(s_PT1, 1)

            def elu_exp(g, p):
                act.wait_ge(s_attn1, g + 1)
                if after(g, 2):
                    act.wait_ge(s_h1, g - 1)
                act.activation(elu_e[p][:, :], pA[:, :], ACT.Exp).then_inc(s_E, 1)

            def score_rows2(g, p):
                act.wait_ge(s_R2, g + 1)
                if after(g, 4):
                    act.wait_ge(s_fin, g - 3)
                act.activation(rows2[p][:, :], pH[0:RW, 256:384], ACT.Copy).then_inc(s_rows2, 1)

            def scaled2(g, p):
                act.wait_ge(s_z2, g + 1)
                if after(g, 2):
                    act.wait_ge(s_P2, g - 1)
                act.activation(L2[p][:, :], pT[:, 384:512], ACT.Copy, scale=SLOPE).then_inc(s_sc2, 1)

            def exp2(g, p):
                act.wait_ge(s_max2, g + 1)
                act.activation(L2[p][:, :], L2[p][:, :], ACT.Exp, bias=nmax2[p][:, :],
                               accum_out=sum2[p][:, :]).then_inc(s_exp2, 1)

            def copy_PT2(g, p):
                act.wait_ge(s_P2T, g + 1)
                if after(g, 2):
                    act.wait_ge(s_attn2, g - 1)
                act.activation(PT2[p][:, :], pS[:, 256:384], ACT.Copy).then_inc(s_PT2, 1)

            def relu_h2(g, p):
                act.wait_ge(s_T2, g + 1)
                if after(g, 2):
                    act.wait_ge(s_h2lo, g - 1)
                    act.wait_ge(s_fin, g - 1)
                psum = pH[:, 0:D].rearrange("p (k n) -> p k n", k=KD)
                act.activation(h2T_f[p][:, :, :], psum, ACT.Relu)
                act.activation(h2T_hi[p][:, :, :], psum, ACT.Relu).then_inc(s_h2hi, 1)

            def high_h1(g, p):
                act.wait_ge(s_h1, g + 1)
                if after(g, 2):
                    act.wait_ge(s_xl2, g - 1)
                act.activation(h1_hi[p][:, :, :].rearrange("p a b -> p (a b)"), h1[p][:, :], ACT.Copy).then_inc(s_h1hi, 1)

            def features2(g, p):
                act.wait_ge(s_ab2, g + 1)
                if after(g, 2):
                    act.wait_ge(s_attn2, g - 1)
                act.activation(xl2[p][:, :], pZ[:, 0:D], ACT.Copy).then_inc(s_xl2sb, 1)

            def high_w1(g, p):
                if not isinstance(g, int) or g:
                    return
                act.wait_ge(s_w1dma, 64)
                act.activation(w1_hi[:, :, :, 0:HALF], w1_f[:, :, :].rearrange("p k (a n) -> p k a n", a=2),
                               ACT.Copy).then_inc(s_w1hi, 1)

            def high_w2(g, p):
                if not isinstance(g, int) or g:
                    return
                act.wait_ge(s_w2dma, 64)
                act.activation(w2_hi[:, :, 0:D], w2_f[:, :, :], ACT.Copy).then_inc(s_w2hi, 1)

            pipeline(act, [(score_rows1, 0), (high_h1, 2), (features2, 3), (score_rows2, 3), (relu_h, -1), (high_w2, 0),
                           (copy_PT1, 1), (scaled1, 0), (place_label_rows, 3), (high_w1, -4), (copy_PT2, 4), (scaled2, 3),
                           (relu_h2, 5), (no_edges, -5), (elu_exp, 1), (exp1, 0), (exp2, 3)])

        @block.vector
        def _(dve):
            prep = [0]

            def link(ins):
                prep[0] += 1
                ins.then_inc(s_prep, 1)
                dve.wait_ge(s_prep, prep[0])

            for p in range(2):
                dve.memset(ab1[p][:, :].bitcast(F32), 0.0)
                dve.memset(ab2[p][:, :].bitcast(F32), 0.0)
            dve.memset(label_rows[:, :].bitcast(F32), 0.0).then_inc(s_consts, 1)
            dve.wait_ge(s_ident, 6)
            dve.tensor_copy(ident_r[:, :], ident[:, :])
            link(dve.tensor_copy(ident_bf[:, :], ident[:, :]))
            link(dve.tensor_tensor(fold[:, :], ident[0:RW, 0:8], ident[0:RW, LO:LO + 8], ALU.add))
            for h in range(H):
                r = row_of(h)
                dve.tensor_copy(sel_src1[:, h, :], fold[:, r:r + 1].broadcast_to([RW, 128]))
                link(dve.tensor_copy(sel_dst1[:, h, :], fold[:, r + 2:r + 3].broadcast_to([RW, 128])))
            dve.tensor_copy(sel_src2[:, :], fold[:, 0:1].broadcast_to([RW, 128]))
            link(dve.tensor_copy(sel_dst2[:, :], fold[:, 1:2].broadcast_to([RW, 128])))
            for p in range(2):
                link(dve.memset(ab2[p][:, 3:RW:LO].bitcast(F32), 1.0))
            dve.tensor_copy(ident_bf[:, 0:1], ident[:, 0:1]).then_inc(s_consts, 1)

            def weigh_w1(g, p):
                if not isinstance(g, int) or g:
                    return
                dve.wait_ge(s_w1dma, 64)
                link(dve.tensor_tensor(w1_att[:, 0, :].rearrange("p (k n) -> p k n", k=KD), w1_f[:, :, :],
                                       att1_bc[:, 0, :].unsqueeze(1).broadcast_to([128, KD, HF]), ALU.mult))
                dve.tensor_reduce(w1_scores[:, 0, :], w1_att[:, 0, :].rearrange("p (m f) -> p m f", f=FH), AX.X, ALU.add)
                dve.wait_ge(s_w1hi, 1)
                for k in range(KD):
                    last = dve.tensor_tensor(w1_lo[:, k, :, 0:HALF], w1_f[:, k, :].rearrange("p (a n) -> p a n", a=2),
                                             w1_hi[:, k, :, 0:HALF].bitcast(F32), ALU.subtract)
                link(last)

            def prepare_w1(g, p):
                if not isinstance(g, int) or g:
                    return
                dve.wait_ge(s_w1att, 1)
                link(dve.tensor_reduce(w1_scores[:, 1, :], w1_att[:, 1, :].rearrange("p (m f) -> p m f", f=FH), AX.X, ALU.add))
                cols = [w1_scores[:, j, :].rearrange("p (m h) -> p m h", h=2) for j in range(2)]
                hi, lo = ([w[:, :, :, HALF + 2 * j:HALF + 2 * j + 2].rearrange("p k a h -> p (k a) h") for j in range(2)]
                          for w in (w1_hi, w1_lo))
                dve.tensor_copy(hi[0], cols[0])
                link(dve.tensor_copy(hi[1], cols[1]))
                dve.tensor_tensor(lo[0], cols[0], hi[0].bitcast(F32), ALU.subtract)
                dve.tensor_tensor(lo[1], cols[1], hi[1].bitcast(F32), ALU.subtract).then_inc(s_w1ready, 1)

            def weigh_w2(g, p):
                if not isinstance(g, int) or g:
                    return
                dve.wait_ge(s_w2dma, 64)
                link(dve.tensor_tensor(w2_att[:, 0, :].rearrange("p (k n) -> p k n", k=KH), w2_f[:, :, :],
                                       att2_bc[:, 0, :].unsqueeze(1).broadcast_to([128, KH, D]), ALU.mult))
                link(dve.tensor_reduce(w2_scores[:, 0, :], w2_att[:, 0, :].rearrange("p (k n) -> p k n", k=KH), AX.X, ALU.add))

            def prepare_w2(g, p):
                if not isinstance(g, int) or g:
                    return
                dve.wait_ge(s_w2att, 1)
                link(dve.tensor_reduce(w2_scores[:, 1, :], w2_att[:, 1, :].rearrange("p (k n) -> p k n", k=KH), AX.X, ALU.add))
                for j in range(2):
                    link(dve.tensor_copy(w2_hi[:, :, D + j], w2_scores[:, j, :]))
                    last = dve.tensor_tensor(w2_lo[:, :, D + j], w2_scores[:, j, :], w2_hi[:, :, D + j].bitcast(F32),
                                             ALU.subtract)
                last.then_inc(s_w2ready, 1)

            def sum_w3(g, p):
                if not isinstance(g, int) or g:
                    return
                dve.wait_ge(s_w3dma, 32)
                link(dve.tensor_tensor(w3_f[:, 0, :, :], w3_f[:, 0, :, :], w3_f[:, 1, :, :], ALU.add))
                for k in range(KD):
                    last = dve.tensor_tensor(w3_f[:, 0, k, k * 128:(k + 1) * 128], w3_f[:, 0, k, k * 128:(k + 1) * 128],
                                             ident[:, :], ALU.add)
                last.then_inc(s_w3ready, 1)

            def label_terms(g, p):
                if not isinstance(g, int) or g:
                    return
                dve.wait_ge(s_labdma, 16)
                dve.tensor_tensor(lab_f[:, 0, :], lab[:, 0, :], lab[:, 1, :], ALU.subtract)
                link(dve.tensor_scalar(lab_f[:, 1, :], lab[:, 1, :], float(N), None, ALU.mult))
                link(dve.tensor_copy(lab_parts[:, 0:2, :], lab_f[:, :, :]))
                dve.tensor_tensor(lab_parts[:, 2:4, :], lab_f[:, :, :], lab_parts[:, 0:2, :].bitcast(F32),
                                  ALU.subtract).then_inc(s_w3ready, 1)

            def split_w3(g, p):
                if not isinstance(g, int) or g:
                    return
                dve.wait_ge(s_w3T, 1)
                w3T = pF[:, :].rearrange("p (k o) -> p k o", k=KD)
                link(dve.tensor_copy(w3_hi[:, :, :], w3T))
                dve.tensor_tensor(w3_lo[:, :, :], w3T, w3_hi[:, :, :].bitcast(F32), ALU.subtract).then_inc(s_w3ready, 1)

            def stats1(g, p):
                dve.wait_ge(s_ident, 6)
                dve.wait_ge(s_loaded, g + 1)
                dve.bn_stats(bn1[:, p % 2, :], of_graph(x_all, g, D)).then_inc(s_bn1, 1)

            def release1(g, p):
                if p % 2 and after(g, 2):
                    dve.wait_ge(s_hn, g - 1)

            def aggregate1(g, p):
                if p % 2 == 0:
                    return
                dve.wait_ge(s_ident, 6)
                dve.wait_ge(s_bn1, g + 1)
                dve.bn_aggr(mv1[:, 0, :], bn1[:, 0, :])
                dve.bn_aggr(mv1[:, 1, :], bn1[:, 1, :]).then_inc(s_mv1, 2)

            def largest_labels(g, p):
                if p % 2 == 0:
                    return
                dve.wait_ge(s_ident, 6)
                dve.wait_ge(s_loaded, g + 1)
                dve.tensor_reduce(of_graph(top_label, (g - 1) // 2, 1), of_graph(adj_all, g - 1, N, 2),
                                  AX.X, ALU.max).then_inc(s_top, 1)

            def largest_of_rows(g, p):
                if not isinstance(g, int) or g != G - 1:
                    return
                dve.wait_ge(s_top, G // 2)
                dve.tensor_reduce(top[:, :], top_label[:, :], AX.X, ALU.max).then_inc(s_top, 1)

            def largest_label(g, p):
                if not isinstance(g, int) or g != G - 1:
                    return
                dve.wait_ge(s_toprow, 1)
                link(dve.tensor_reduce(top_row[:, :], pX[0:1, 0, 0:128], AX.X, ALU.max))
                dve.tensor_copy(top_int[:, :], top_row[:, :]).then_inc(s_label, 1)

            def layer_norm1(g, p):
                dve.wait_ge(s_rs1, g + 1)
                if after(g, 2):
                    dve.wait_ge(s_T0, g - 1)
                dve.tensor_scalar(hn[p][:, :], of_graph(x_all, g, D), mv1[:, p % 2, 0:1], rstd1[:, p % 2:p % 2 + 1],
                                  ALU.subtract, ALU.mult).then_inc(s_hn, 1)

            def layer_norm2(g, p):
                dve.wait_ge(s_rs2, g + 1)
                if after(g, 2):
                    dve.wait_ge(s_T2, g - 1)
                dve.tensor_scalar(h2n[p][:, :], of_graph(x_all, g, D), mv2[p][:, 0:1], rstd2[:, :],
                                  ALU.subtract, ALU.mult).then_inc(s_h2n, 1)

            def high_scores1(g, p):
                dve.wait_ge(s_xl1, g + 1)
                dve.tensor_copy(ab1[p][:, 0:8].rearrange("p (a c) -> p a c", a=2), pX[:, :, HALF:C1]).then_inc(s_ab1hi, 1)

            def low_scores1(g, p):
                dve.wait_ge(s_ab1hi, g + 1)
                dve.tensor_tensor(ab1[p][:, LO:LO + 8].rearrange("p (a c) -> p a c", a=2), pX[:, :, HALF:C1],
                                  ab1[p][:, 0:8].rearrange("p (a c) -> p a c", a=2).bitcast(F32),
                                  ALU.subtract).then_inc(s_ab1, 1)

            def features1(g, p):
                if after(g, 2):
                    dve.wait_ge(s_attn1, g - 1)
                dve.tensor_tensor(xl[p][:, :].rearrange("p (a n) -> p a n", a=2), pX[:, :, 0:HALF],
                                  b1_bc[:, :].rearrange("p (a n) -> p a n", a=2), ALU.add).then_inc(s_xlsb, 1)

            def leaky1(g, p):
                dve.wait_ge(s_sc1, g + 1)
                dve.tensor_tensor(L1[p][:, :, :].rearrange("p h s -> p (h s)"), pZ[:, :],
                                  L1[p][:, :, :].rearrange("p h s -> p (h s)"), ALU.max).then_inc(s_L1, 1)

            def max1(g, p):
                dve.wait_ge(s_L1, g + 1)
                dve.tensor_reduce(nmax1[p][:, :], L1[p][:, :, :], AX.X, ALU.max, negate=True).then_inc(s_max1, 1)

            def recip1(g, p):
                dve.wait_ge(s_exp1, g + 1)
                dve.reciprocal(rsum1[p][:, :], sum1[p][:, :]).then_inc(s_rsum1, 1)

            def elu_clamp(g, p):
                dve.wait_ge(s_E, g + 1)
                dve.tensor_scalar(elu_e[p][:, :], elu_e[p][:, :], 1.0, -1.0, ALU.min, ALU.add).then_inc(s_elu_a, 1)

            def elu_max(g, p):
                dve.wait_ge(s_elu_a, g + 1)
                if after(g, 2):
                    dve.wait_ge(s_h1lo, g - 1)
                dve.tensor_tensor(h1[p][:, :], pA[:, :], elu_e[p][:, :], ALU.max).then_inc(s_h1, 1)

            def scores2(g, p):
                dve.wait_ge(s_xl2, g + 1)
                dve.tensor_copy(ab2[p][:, 0:2], pZ[:, D:C2]).then_inc(s_ab2hi, 1)
                dve.tensor_copy(ab2[p][:, 2:RW:LO], of_graph(n0_all, g, 1).broadcast_to([128, 2])).then_inc(s_n0col, 1)
                dve.wait_ge(s_ab2hi, g + 1)
                dve.tensor_tensor(ab2[p][:, LO:LO + 2], pZ[:, D:C2], ab2[p][:, 0:2].bitcast(F32),
                                  ALU.subtract).then_inc(s_ab2, 1)

            def leaky2(g, p):
                dve.wait_ge(s_sc2, g + 1)
                dve.tensor_tensor(L2[p][:, :], pT[:, 384:512], L2[p][:, :], ALU.max).then_inc(s_L2, 1)

            def max2(g, p):
                dve.wait_ge(s_L2, g + 1)
                dve.tensor_reduce(nmax2[p][:, :], L2[p][:, :], AX.X, ALU.max, negate=True).then_inc(s_max2, 1)

            def recip2(g, p):
                dve.wait_ge(s_exp2, g + 1)
                dve.reciprocal(rsum2[p][:, :], sum2[p][:, :]).then_inc(s_rsum2, 1)

            def normalise2(g, p):
                dve.wait_ge(s_rsum2, g + 1)
                if after(g, 2):
                    dve.wait_ge(s_P2T, g - 1)
                dve.tensor_scalar(P2[p][:, :], L2[p][:, :], rsum2[p][:, :], None, ALU.mult).then_inc(s_P2, 1)

            def residual1(g, p):
                dve.wait_ge(s_attn2, g + 1)
                dve.wait_ge(s_xb, g + 1)
                if after(g, 2):
                    dve.wait_ge(s_h2n, g - 1)
                dve.tensor_tensor(of_graph(x_all, g, D), pS[:, 0:D], of_graph(x_all, g, D), ALU.add).then_inc(s_x2, 1)

            def stats2(g, p):
                dve.wait_ge(s_ident, 6)
                dve.wait_ge(s_x2, g + 1)
                dve.bn_stats(bn2[:, :], of_graph(x_all, g, D)).then_inc(s_bn2, 1)

            def aggregate2(g, p):
                dve.wait_ge(s_ident, 6)
                dve.wait_ge(s_bn2, g + 1)
                dve.bn_aggr(mv2[p][:, :], bn2[:, :]).then_inc(s_mv2, 1)

            def residual2(g, p):
                dve.wait_ge(s_fin, g + 1)
                dve.wait_ge(s_h2n, g + 1)
                dve.tensor_tensor(of_graph(x_all, g, D), pF[:, 0:D], of_graph(x_all, g, D), ALU.add).then_inc(s_out, 1)

            pipeline(dve, [(leaky1, 0), (max1, 0), (sum_w3, 1), (leaky2, 3), (residual1, 4), (max2, 3), (stats2, 4),
                           (elu_clamp, 1), (aggregate2, 4), (high_scores1, -1), (largest_labels, -1), (low_scores1, -1),
                           (recip1, 0), (elu_max, 1), (scores2, 2), (recip2, 3), (normalise2, 3), (layer_norm1, -3),
                           (weigh_w1, -3), (prepare_w1, -3), (features1, -1), (weigh_w2, -1), (prepare_w2, 0),
                           (label_terms, 1), (layer_norm2, 4), (stats1, -5), (release1, -5), (residual2, 5), (split_w3, 4),
                           (aggregate1, -5), (largest_of_rows, 1), (largest_label, 4)])

            dve.wait_ge(s_label, 1)
            labelled = dve.value_load(top_int[0:1, 0:1], min_val=0, max_val=LABELS - 1)
            with dve.If(labelled > 1):
                for j in range(LABELS - 2):
                    link(dve.memset(label_no[:, j:j + 1], float(j + 2)))
                dve.wait_ge(s_biasdma, 16)
                dve.tensor_tensor(bias_bc[:, 2:, :], bias_bc[:, 2:, :],
                                  bias_bc[:, 1:2, :].broadcast_to([128, LABELS - 2, D]), ALU.subtract).then_inc(s_diff, 1)
                dve.wait_ge(s_diff, 1)
                with dve.Fori(0, G) as g:
                    dve.tensor_tensor(is_label[:, :, :], of_graph(adj_all, g, N).unsqueeze(1).broadcast_to([128, LABELS - 2, N]),
                                      label_no[:, :].unsqueeze(2).broadcast_to([128, LABELS - 2, N]),
                                      ALU.is_equal).then_inc(s_fixed, 1)
                    dve.wait_ge(s_fixed, FIX * g + 1)
                    dve.tensor_reduce(label_count[:, :], is_label[:, :, :], AX.X, ALU.add).then_inc(s_fixed, 1)
                    for j in range(LABELS - 2):
                        dve.wait_ge(s_fixed, FIX * g + 2 + j)
                        dve.scalar_tensor_tensor(of_graph(x_all, g, D), bias_bc[:, j + 2, :], label_count[:, j:j + 1],
                                                 of_graph(x_all, g, D), ALU.mult, ALU.add).then_inc(s_fixed, 1)

        @block.tensor
        def _(pe):
            pe.wait_ge(s_consts, 2)

            def transpose_w3(g, p):
                if not isinstance(g, int) or g:
                    return
                pe.wait_ge(s_w3ready, 1)
                for ki in range(KD):
                    for ko in range(KD):
                        mm = pe.transpose(pF[:, ki * D + ko * 128:ki * D + (ko + 1) * 128],
                                          w3_f[:, 0, ko, ki * 128:(ki + 1) * 128], ident[:, :])
                mm.then_inc(s_w3T, 1)

            def transpose_h(g, p):
                pe.wait_ge(s_hn, g + 1)
                if alone(g):
                    pe.wait_ge(s_hThi, g)
                if after(g, 6):
                    pe.wait_ge(s_x2, g - 5)
                for k in range(KD):
                    mm = pe.transpose(pS[:, k * 128:(k + 1) * 128], hn[p][:, k * 128:(k + 1) * 128], ident[:, :])
                mm.then_inc(s_T0, 1)

            def project1(g, p):
                if isinstance(g, int) and g == 0:
                    pe.wait_ge(s_w1ready, 1)
                pe.wait_ge(s_hTlo, g + 1)
                if after(g, 1):
                    pe.wait_ge(s_xlsb, g)
                for a in range(2):
                    for k in range(KD):
                        pe.matmul(pX[:, a, 0:C1], hT_hi[p][:, k, :], w1_hi[:, k, a, :], start=(k == 0), stop=False)
                        pe.matmul(pX[:, a, 0:C1], hT_hi[p][:, k, :], w1_lo[:, k, a, :], start=False, stop=False)
                        mm = pe.matmul(pX[:, a, 0:C1], hT_lo[p][:, k, :], w1_hi[:, k, a, :], start=False, stop=(k == KD - 1))
                mm.then_inc(s_xl1, 1)

            def transpose_scores1(g, p):
                pe.wait_ge(s_ab1, g + 1)
                if alone(g):
                    pe.wait_ge(s_rows1, g)
                if after(g, 4):
                    pe.wait_ge(s_L2, g - 3)
                pe.matmul(pT[0:CW, 128:256], ab1[p][:, :], ident_r[:, :], start=True, stop=True).then_inc(s_R1, 1)

            def scores1(g, p):
                pe.wait_ge(s_rows1, g + 1)
                if alone(g):
                    pe.wait_ge(s_L1, g)
                if after(g, 3):
                    pe.wait_ge(s_xl2sb, g - 2)
                pe.matmul(pZ[:, :], rows1[p][:, :], sel_dst1[:, :, :].rearrange("p h s -> p (h s)"), start=True, stop=False)
                pe.wait_ge(s_mask, g + 1)
                pe.matmul(pZ[:, :].rearrange("p (h s) -> p h s", h=H), of_graph(mask_all, g, N),
                          ident_bf[:, :].unsqueeze(1).broadcast_to([128, H, 128]), start=False, stop=False)
                for h in range(H):
                    mm = pe.matmul(pZ[:, h * 128:(h + 1) * 128], sel_src1[:, h, :], rows1[p][:, :], start=False, stop=(h == H - 1))
                mm.then_inc(s_z1, 1)

            def transpose_P1(g, p):
                pe.wait_ge(s_P1, g + 1)
                if after(g, 1):
                    pe.wait_ge(s_h1, g)
                for h in range(H):
                    mm = pe.transpose(pA[:, h * 128:(h + 1) * 128], P1[p][:, h, :], ident[:, :])
                mm.then_inc(s_PT, 1)

            def attend1(g, p):
                pe.wait_ge(s_PT1, g + 1)
                if alone(g, 0):
                    pe.wait_ge(s_xlsb, g + 1)
                for h in range(H):
                    mm = pe.matmul(pA[:, h * 128:(h + 1) * 128], xl[p][:, h * FH:(h + 1) * FH], PT1[p][:, h, :],
                                   start=True, stop=True)
                mm.then_inc(s_attn1, 1)

            def project2(g, p):
                if isinstance(g, int) and g == 0:
                    pe.wait_ge(s_w2ready, 1)
                    pe.wait_ge(s_w2lo, 1)
                pe.wait_ge(s_h1lo, g + 1)
                if alone(g):
                    pe.wait_ge(s_xl2sb, g)
                pe.wait_ge(s_L1, upto(g, 3))
                for k in range(KH):
                    pe.matmul(pZ[:, 0:C2], h1_hi[p][:, k, :], w2_hi[:, k, :], start=(k == 0), stop=False)
                    pe.matmul(pZ[:, 0:C2], h1_hi[p][:, k, :], w2_lo[:, k, :], start=False, stop=False)
                    mm = pe.matmul(pZ[:, 0:C2], h1_lo[p][:, k, :], w2_hi[:, k, :], start=False, stop=(k == KH - 1))
                mm.then_inc(s_xl2, 1)

            def transpose_scores2(g, p):
                pe.wait_ge(s_ab2, g + 1)
                pe.wait_ge(s_n0col, g + 1)
                if alone(g):
                    pe.wait_ge(s_rows2, g)
                if after(g, 3):
                    pe.wait_ge(s_h2hi, g - 2)
                pe.matmul(pH[0:CW, 256:384], ab2[p][:, :], ident_r[:, :], start=True, stop=True).then_inc(s_R2, 1)

            def scores2(g, p):
                pe.wait_ge(s_rows2, g + 1)
                if alone(g, 0):
                    pe.wait_ge(s_rows1, upto(g, 4))
                if alone(g):
                    pe.wait_ge(s_L2, g)
                z2 = pT[:, 384:512]
                pe.matmul(z2, rows2[p][:, :], sel_dst2[:, :], start=True, stop=False)
                pe.matmul(z2, of_graph(mask_all, g, N), ident_bf[:, :], start=False, stop=False)
                pe.matmul(z2, sel_src2[:, :], rows2[p][:, :], start=False, stop=True).then_inc(s_z2, 1)

            def transpose_P2(g, p):
                pe.wait_ge(s_P2, g + 1)
                pe.wait_ge(s_hThi, upto(g, 6))
                if alone(g):
                    pe.wait_ge(s_x2, g)
                pe.transpose(pS[:, 256:384], P2[p][:, :], ident[:, :]).then_inc(s_P2T, 1)

            def attend2(g, p):
                pe.wait_ge(s_PT2, g + 1)
                if alone(g, 0):
                    pe.wait_ge(s_xl2sb, g + 1)
                pe.matmul(pS[:, 0:D], PT2[p][:, :], xl2[p][:, :], start=True, stop=True).then_inc(s_attn2, 1)

            def transpose_h2(g, p):
                pe.wait_ge(s_h2n, g + 1)
                pe.wait_ge(s_rows2, upto(g, 3))
                if alone(g):
                    pe.wait_ge(s_h2hi, g)
                for k in range(KD):
                    mm = pe.transpose(pH[:, k * 128:(k + 1) * 128], h2n[p][:, k * 128:(k + 1) * 128], ident[:, :])
                mm.then_inc(s_T2, 1)

            def convolve(g, p):
                if isinstance(g, int) and g == 0:
                    pe.wait_ge(s_w3ready, 3)
                    pe.wait_ge(s_labrow, 32)
                pe.wait_ge(s_h2lo, g + 1)
                if after(g, 1):
                    pe.wait_ge(s_out, g)
                for k in range(KD):
                    pe.matmul(pF[:, 0:D], h2T_hi[p][:, k, :], w3_hi[:, k, :], start=(k == 0), stop=False)
                    pe.matmul(pF[:, 0:D], h2T_hi[p][:, k, :], w3_lo[:, k, :], start=False, stop=False)
                    pe.matmul(pF[:, 0:D], h2T_lo[p][:, k, :], w3_hi[:, k, :], start=False, stop=False)
                pe.matmul(pF[:, 0:D], rows2[p][:, :], label_rows[:, :], start=False, stop=True).then_inc(s_fin, 1)

            def gather_top_label(g, p):
                if not isinstance(g, int) or g != G - 1:
                    return
                pe.wait_ge(s_top, G // 2 + 1)
                pe.wait_ge(s_xlsb, G)
                pe.matmul(pX[0:1, 0, 0:128], top[:, :], ident[:, :], start=True, stop=True).then_inc(s_toprow, 1)

            pipeline(pe, [(project1, 0), (transpose_h, -1), (project2, 3), (transpose_scores1, 0), (convolve, 6),
                          (transpose_w3, 4), (transpose_scores2, 3), (transpose_P1, 1), (scores1, 0), (transpose_P2, 4),
                          (scores2, 3), (transpose_h2, 5), (attend1, 1), (attend2, 4), (gather_top_label, 2)])


_INS = ["x", "adj", "L0_gnn_W1", "L0_gnn_att_src1", "L0_gnn_att_dst1", "L0_gnn_b1", "L0_gnn_W2", "L0_gnn_att_src2",
        "L0_gnn_att_dst2", "L0_gnn_b2", "L1_gnn_weights", "L1_gnn_bias"]


def kernel(**inputs):
    import numpy as np
    import concourse.bacc as bacc
    from concourse.bass_utils import run_bass_kernel_spmd

    nc = bacc.Bacc("TRN2", target_bir_lowering=False, num_devices=1)
    arrays, args = {}, []
    for name in _INS:
        a = np.ascontiguousarray(inputs[name])
        arrays[f"in_{name}"] = a
        args.append(nc.dram_tensor(f"in_{name}", a.shape, mybir.dt.from_np(a.dtype), kind="ExternalInput").ap())
    args.append(nc.dram_tensor("out", inputs["x"].shape, mybir.dt.float32, kind="ExternalOutput").ap())
    gat_graphconv_block(nc, *args)
    r = run_bass_kernel_spmd(nc, [arrays], core_ids=[0])
    return r.results[0]["out"]
```
